# Optimizing a Trainium2 kernel written in Bass

```python
import numpy as np
import jax
import jax.numpy as jnp

def _softmax(x, axis=-1):
    return jax.nn.softmax(x, axis=axis)

def _gelu(x):
    return jax.nn.gelu(x, approximate=True)

def _silu(x):
    return jax.nn.silu(x)

def _sigmoid(x):
    return jax.nn.sigmoid(x)

def _layernorm(x, axis=-1, eps=1e-05):
    m = jnp.mean(x, axis=axis, keepdims=True)
    v = jnp.var(x, axis=axis, keepdims=True)
    return (x - m) / jnp.sqrt(v + eps)

def _scatter_add(tgt, idx, src, axis=0):
    return tgt.at[idx].add(src)

def _segment_sum(src, seg, n):
    return jax.ops.segment_sum(src, seg, n)
kernel_name = 'mk_early_fusion_d2_tok_img768_r4_2fb372'

def setup_inputs(seed: int=0):
    np.random.seed(seed)
    _w = jnp.asarray

    def _rec_inputs():
        import jax
        import jax.numpy as jnp
        _rk = jax.random.key(seed)
        x = 7.57192e-06 + 1.00007 * jax.random.normal(jax.random.fold_in(_rk, 1), (32, 96, 96, 3), jnp.float32)
        txt = -0.0429142 + 10 * jax.random.normal(jax.random.fold_in(_rk, 2), (32, 77, 192), jnp.float32)
        return (x, txt)
    x, txt = _rec_inputs()

    def _L0_tok_setup():
        import jax, jax.numpy as jnp
        import numpy as np
        PATCH = 16
        DIM = 192
        EPS = 0.001

        def _shifts(x):
            zw = jnp.zeros_like(x[:, :, :1, :])
            right = jnp.concatenate([zw, x[:, :, :-1, :]], axis=2)
            left = jnp.concatenate([x[:, :, 1:, :], zw], axis=2)
            zh = jnp.zeros_like(x[:, :1, :, :])
            down = jnp.concatenate([zh, x[:, :-1, :, :]], axis=1)
            up = jnp.concatenate([x[:, 1:, :, :], zh], axis=1)
            return [right, left, down, up]

        def _patchify(x, p):
            b, H, W, C = x.shape
            hh, ww = (H // p, W // p)
            x = x.reshape(b, hh, p, ww, p, C)
            x = x.transpose(0, 1, 3, 2, 4, 5)
            return x.reshape(b, hh * ww, p * p * C)
        key = jax.random.key(seed)
        k1, k2 = jax.random.split(key)
        b, H, Wd, C = (64, 224, 224, 3)
        F = PATCH * PATCH * 5 * C
        x = jax.random.normal(k1, (b, H, Wd, C), dtype=jnp.float32)
        gamma = jnp.ones((F,), dtype=jnp.float32)
        beta = jnp.zeros((F,), dtype=jnp.float32)
        W = jax.random.normal(k2, (F, DIM), dtype=jnp.float32)
        bb = jnp.zeros((DIM,), dtype=jnp.float32)
        return {'x': x, 'gamma': gamma, 'beta': beta, 'W': W, 'b': bb}
    _L0_tok_all = _L0_tok_setup()
    _L0_tok_in = {k: v for k, v in _L0_tok_all.items() if k in ('gamma', 'beta', 'W', 'b')}
    del _L0_tok_all

    def _L0_attn_setup():
        import jax, jax.numpy as jnp
        import numpy as np
        DIM = 192
        NUM_HEADS = 12
        HEAD_DIM = DIM // NUM_HEADS
        SCALE = HEAD_DIM ** (-0.5)
        key = jax.random.key(seed)
        k_x, k_qkv, k_proj, k_pb = jax.random.split(key, 4)
        B, N = (8, 256)
        x = jax.random.normal(k_x, (B, N, DIM), dtype=jnp.float32)
        w_qkv = jax.random.normal(k_qkv, (3 * DIM, DIM), dtype=jnp.float32) * DIM ** (-0.5)
        w_proj = jax.random.normal(k_proj, (DIM, DIM), dtype=jnp.float32) * DIM ** (-0.5)
        b_proj = jax.random.normal(k_pb, (DIM,), dtype=jnp.float32) * 0.01
        return {'x': x, 'w_qkv': w_qkv, 'w_proj': w_proj, 'b_proj': b_proj}
    _L0_attn_all = _L0_attn_setup()
    _L0_attn_in = {k: v for k, v in _L0_attn_all.items() if k in ('w_qkv', 'w_proj', 'b_proj')}
    del _L0_attn_all

    def _L0_ffn_setup():
        import jax, jax.numpy as jnp
        import numpy as np
        B, N, D, E, F, K = (2, 512, 192, 8, 768, 2)
        V_MAX = 3.0
        FEAT_CLAMP = 10.0

        def bk_green_diag(a):
            aT = jnp.swapaxes(a, 0, 1)

            def step(c, ai):
                d = ai - 1.0 / c
                return (d, d)
            d0 = aT[0]
            _, d_rest = jax.lax.scan(step, d0, aT[1:])
            d = jnp.concatenate([d0[None], d_rest], axis=0)
            eN = aT[-1]
            _, e_rest = jax.lax.scan(step, eN, aT[:-1], reverse=True)
            e = jnp.concatenate([e_rest, eN[None]], axis=0)
            G = 1.0 / (d + e - aT)
            return jnp.swapaxes(G, 0, 1)
        key = jax.random.key(seed)
        ks = jax.random.split(key, 8)
        s = lambda k, shape, sc: jax.random.normal(k, shape, jnp.float32) * sc
        return {'x': s(ks[0], (B, N, D), 1.0), 'v_w': s(ks[1], (D,), 0.02), 'v_b': jnp.zeros((), jnp.float32), 'gate_w': s(ks[2], (D, E), 0.02), 'gate_b': jnp.zeros((E,), jnp.float32), 'w1': s(ks[3], (E, D, F), 0.02), 'b1': jnp.zeros((E, F), jnp.float32), 'w2': s(ks[4], (E, F, D), 0.02), 'b2': jnp.zeros((E, D), jnp.float32), 'out_w': s(ks[5], (2, D), 0.02), 'out_b': jnp.zeros((D,), jnp.float32), 'bk_scale': jnp.ones((D,), jnp.float32)}
    _L0_ffn_all = _L0_ffn_setup()
    _L0_ffn_in = {k: v for k, v in _L0_ffn_all.items() if k in ('v_w', 'v_b', 'gate_w', 'gate_b', 'w1', 'b1', 'w2', 'b2', 'out_w', 'out_b', 'bk_scale')}
    del _L0_ffn_all

    def _L1_attn_setup():
        import jax, jax.numpy as jnp
        import numpy as np
        NUM_HEADS = 12

        @jax.custom_vjp
        def ste_sign(x):
            return jnp.where(x >= 0, 1.0, -1.0).astype(x.dtype)

        def _ste_sign_fwd(x):
            return (ste_sign(x), x)

        def _ste_sign_bwd(x, g):
            return (g * (jnp.abs(x) <= 1.0).astype(g.dtype),)
        ste_sign.defvjp(_ste_sign_fwd, _ste_sign_bwd)

        def binary_linear_adapscaling(x, w, b=None):
            scale = jax.lax.stop_gradient(jnp.mean(jnp.abs(w), axis=1, keepdims=True))
            bw = ste_sign(w) * scale
            y = jnp.einsum('bnc,oc->bno', x, bw)
            if b is not None:
                y = y + b
            return y
        key = jax.random.key(seed)
        k1, k2, k3 = jax.random.split(key, 3)
        B, N, C = (8, 256, 192)
        x = jax.random.normal(k1, (B, N, C), jnp.float32)
        w_qkv = jax.random.normal(k2, (3 * C, C), jnp.float32) * 0.02
        w_proj = jax.random.normal(k3, (C, C), jnp.float32) * 0.02
        b_proj = jnp.zeros((C,), jnp.float32)
        return {'x': x, 'w_qkv': w_qkv, 'w_proj': w_proj, 'b_proj': b_proj}
    _L1_attn_all = _L1_attn_setup()
    _L1_attn_in = {k: v for k, v in _L1_attn_all.items() if k in ('w_qkv', 'w_proj', 'b_proj')}
    del _L1_attn_all

    def _L1_ffn_setup():
        import jax, jax.numpy as jnp
        import numpy as np
        D_MODEL = 192
        N_EXPERTS = 8
        TOP_K = 2
        D_FF = 4 * D_MODEL
        key = jax.random.key(seed)
        ks = jax.random.split(key, 6)
        B, S = (2, 512)
        x = jax.random.normal(ks[0], (B, S, D_MODEL), dtype=jnp.float32)
        Wr = jax.random.normal(ks[1], (D_MODEL, N_EXPERTS), dtype=jnp.float32) * 0.02
        W1 = jax.random.normal(ks[2], (N_EXPERTS, D_MODEL, D_FF), dtype=jnp.float32) * 0.02
        b1 = jnp.zeros((N_EXPERTS, D_FF), dtype=jnp.float32)
        W2 = jax.random.normal(ks[3], (N_EXPERTS, D_FF, D_MODEL), dtype=jnp.float32) * 0.02
        b2 = jnp.zeros((N_EXPERTS, D_MODEL), dtype=jnp.float32)
        return {'x': x, 'Wr': Wr, 'W1': W1, 'b1': b1, 'W2': W2, 'b2': b2}
    _L1_ffn_all = _L1_ffn_setup()
    _L1_ffn_in = {k: v for k, v in _L1_ffn_all.items() if k in ('Wr', 'W1', 'b1', 'W2', 'b2')}
    del _L1_ffn_all
    return {'x': x, 'txt': txt, 'L0_tok_gamma': _L0_tok_in['gamma'], 'L0_tok_beta': _L0_tok_in['beta'], 'L0_tok_W': _L0_tok_in['W'], 'L0_tok_b': _L0_tok_in['b'], 'L0_attn_w_qkv': _L0_attn_in['w_qkv'], 'L0_attn_w_proj': _L0_attn_in['w_proj'], 'L0_attn_b_proj': _L0_attn_in['b_proj'], 'L0_ffn_v_w': _L0_ffn_in['v_w'], 'L0_ffn_v_b': _L0_ffn_in['v_b'], 'L0_ffn_gate_w': _L0_ffn_in['gate_w'], 'L0_ffn_gate_b': _L0_ffn_in['gate_b'], 'L0_ffn_w1': _L0_ffn_in['w1'], 'L0_ffn_b1': _L0_ffn_in['b1'], 'L0_ffn_w2': _L0_ffn_in['w2'], 'L0_ffn_b2': _L0_ffn_in['b2'], 'L0_ffn_out_w': _L0_ffn_in['out_w'], 'L0_ffn_out_b': _L0_ffn_in['out_b'], 'L0_ffn_bk_scale': _L0_ffn_in['bk_scale'], 'L1_attn_w_qkv': _L1_attn_in['w_qkv'], 'L1_attn_w_proj': _L1_attn_in['w_proj'], 'L1_attn_b_proj': _L1_attn_in['b_proj'], 'L1_ffn_Wr': _L1_ffn_in['Wr'], 'L1_ffn_W1': _L1_ffn_in['W1'], 'L1_ffn_b1': _L1_ffn_in['b1'], 'L1_ffn_W2': _L1_ffn_in['W2'], 'L1_ffn_b2': _L1_ffn_in['b2']}

def reference(x, txt, L0_tok_gamma, L0_tok_beta, L0_tok_W, L0_tok_b, L0_attn_w_qkv, L0_attn_w_proj, L0_attn_b_proj, L0_ffn_v_w, L0_ffn_v_b, L0_ffn_gate_w, L0_ffn_gate_b, L0_ffn_w1, L0_ffn_b1, L0_ffn_w2, L0_ffn_b2, L0_ffn_out_w, L0_ffn_out_b, L0_ffn_bk_scale, L1_attn_w_qkv, L1_attn_w_proj, L1_attn_b_proj, L1_ffn_Wr, L1_ffn_W1, L1_ffn_b1, L1_ffn_W2, L1_ffn_b2):
    import jax
    import jax.numpy as jnp

    def _L0_tok_ref(x, gamma, beta, W, b):
        import jax, jax.numpy as jnp
        import numpy as np
        PATCH = 16
        DIM = 192
        EPS = 0.001

        def _shifts(x):
            zw = jnp.zeros_like(x[:, :, :1, :])
            right = jnp.concatenate([zw, x[:, :, :-1, :]], axis=2)
            left = jnp.concatenate([x[:, :, 1:, :], zw], axis=2)
            zh = jnp.zeros_like(x[:, :1, :, :])
            down = jnp.concatenate([zh, x[:, :-1, :, :]], axis=1)
            up = jnp.concatenate([x[:, 1:, :, :], zh], axis=1)
            return [right, left, down, up]

        def _patchify(x, p):
            b, H, W, C = x.shape
            hh, ww = (H // p, W // p)
            x = x.reshape(b, hh, p, ww, p, C)
            x = x.transpose(0, 1, 3, 2, 4, 5)
            return x.reshape(b, hh * ww, p * p * C)
        x5 = jnp.concatenate([x] + _shifts(x), axis=-1)
        tokens = _patchify(x5, PATCH)
        mu = jnp.mean(tokens, axis=-1, keepdims=True)
        var = jnp.mean(jnp.square(tokens - mu), axis=-1, keepdims=True)
        ln = (tokens - mu) * jax.lax.rsqrt(var + EPS) * gamma + beta
        return jnp.einsum('bnf,fd->bnd', ln, W) + b

    def _L0_attn_ref(x, w_qkv, w_proj, b_proj):
        import jax, jax.numpy as jnp
        import numpy as np
        DIM = 192
        NUM_HEADS = 12
        HEAD_DIM = DIM // NUM_HEADS
        SCALE = HEAD_DIM ** (-0.5)
        B, N, C = x.shape
        H, D = (NUM_HEADS, HEAD_DIM)
        qkv = jnp.einsum('bnc,oc->bno', x, w_qkv)
        qkv = qkv.reshape(B, N, 3, H, D).transpose(2, 0, 3, 1, 4)
        q, k, v = (qkv[0], qkv[1], qkv[2])
        attn = jnp.einsum('bhnd,bhmd->bhnm', q.astype(jnp.float32), k.astype(jnp.float32)) * SCALE
        attn = jax.nn.softmax(attn, axis=-1)
        attn = jnp.where(jnp.isnan(attn), 0.0, attn)
        out = jnp.einsum('bhnm,bhmd->bhnd', attn, v.astype(jnp.float32))
        out = out.transpose(0, 2, 1, 3).reshape(B, N, C)
        out = jnp.einsum('bnc,oc->bno', out, w_proj) + b_proj
        return out

    def _L0_ffn_ref(x, v_w, v_b, gate_w, gate_b, w1, b1, w2, b2, out_w, out_b, bk_scale):
        import jax, jax.numpy as jnp
        import numpy as np
        B, N, D, E, F, K = (2, 512, 192, 8, 768, 2)
        V_MAX = 3.0
        FEAT_CLAMP = 10.0

        def bk_green_diag(a):
            aT = jnp.swapaxes(a, 0, 1)

            def step(c, ai):
                d = ai - 1.0 / c
                return (d, d)
            d0 = aT[0]
            _, d_rest = jax.lax.scan(step, d0, aT[1:])
            d = jnp.concatenate([d0[None], d_rest], axis=0)
            eN = aT[-1]
            _, e_rest = jax.lax.scan(step, eN, aT[:-1], reverse=True)
            e = jnp.concatenate([e_rest, eN[None]], axis=0)
            G = 1.0 / (d + e - aT)
            return jnp.swapaxes(G, 0, 1)
        v = jnp.clip(x @ v_w + v_b, -V_MAX, V_MAX)
        a = (-2.0 + v).astype(jnp.complex64) - 1j
        G = bk_green_diag(a)
        feats = jnp.stack([G.real, G.imag], axis=-1)
        logits = x @ gate_w + gate_b
        probs = jax.nn.softmax(logits, axis=-1)
        topv, topi = jax.lax.top_k(probs, K)
        topv = topv / jnp.sum(topv, axis=-1, keepdims=True)
        comb = jnp.sum(topv[..., None] * jax.nn.one_hot(topi, E, dtype=x.dtype), axis=2)
        h = jax.nn.gelu(jnp.einsum('bnd,edf->bnef', x, w1) + b1)
        y = jnp.einsum('bnef,efd->bned', h, w2) + b2
        ffn_out = jnp.einsum('bne,bned->bnd', comb, y)
        feats_c = jnp.clip(feats, -FEAT_CLAMP, FEAT_CLAMP)
        spec_out = feats_c @ out_w + out_b
        return ffn_out + bk_scale * spec_out

    def _L1_attn_ref(x, w_qkv, w_proj, b_proj):
        import jax, jax.numpy as jnp
        import numpy as np
        NUM_HEADS = 12

        @jax.custom_vjp
        def ste_sign(x):
            return jnp.where(x >= 0, 1.0, -1.0).astype(x.dtype)

        def _ste_sign_fwd(x):
            return (ste_sign(x), x)

        def _ste_sign_bwd(x, g):
            return (g * (jnp.abs(x) <= 1.0).astype(g.dtype),)
        ste_sign.defvjp(_ste_sign_fwd, _ste_sign_bwd)

        def binary_linear_adapscaling(x, w, b=None):
            scale = jax.lax.stop_gradient(jnp.mean(jnp.abs(w), axis=1, keepdims=True))
            bw = ste_sign(w) * scale
            y = jnp.einsum('bnc,oc->bno', x, bw)
            if b is not None:
                y = y + b
            return y
        B, N, C = x.shape
        H = NUM_HEADS
        D = C // H
        scale = D ** (-0.5)
        qkv = binary_linear_adapscaling(x, w_qkv)
        qkv = qkv.reshape(B, N, 3, H, D).transpose(2, 0, 3, 1, 4)
        bqkv = ste_sign(qkv)
        q, k, v = (bqkv[0], bqkv[1], bqkv[2])
        attn = jnp.einsum('bhnd,bhmd->bhnm', q, k) * scale
        soft = jax.nn.softmax(attn, axis=-1)
        binq = (attn > 0).astype(attn.dtype)
        attn = jax.lax.stop_gradient(binq - soft) + soft
        out = jnp.einsum('bhnm,bhmd->bhnd', attn, v)
        out = out.transpose(0, 2, 1, 3).reshape(B, N, C)
        out = binary_linear_adapscaling(out, w_proj, b_proj)
        return out

    def _L1_ffn_ref(x, Wr, W1, b1, W2, b2):
        import jax, jax.numpy as jnp
        import numpy as np
        D_MODEL = 192
        N_EXPERTS = 8
        TOP_K = 2
        D_FF = 4 * D_MODEL
        B, S, D = x.shape
        T = B * S
        x_flat = x.reshape(T, D)
        gate_logits = x_flat @ Wr
        topw, topi = jax.lax.top_k(gate_logits, TOP_K)
        topw = jax.nn.softmax(topw, axis=-1)
        combine = jnp.zeros((T, N_EXPERTS), dtype=x.dtype)
        combine = combine.at[jnp.arange(T)[:, None], topi].add(topw)
        h = jax.nn.relu(jnp.einsum('td,edh->eth', x_flat, W1) + b1[:, None, :])
        y = jnp.einsum('eth,ehd->etd', h, W2) + b2[:, None, :]
        out = jnp.einsum('te,etd->td', combine, y)
        return out.reshape(B, S, D)
    h = _L0_tok_ref(x, L0_tok_gamma, L0_tok_beta, L0_tok_W, L0_tok_b)
    h = jnp.concatenate([h, txt], axis=1)
    h = h + _L0_attn_ref(_layernorm(h, axis=-1), L0_attn_w_qkv, L0_attn_w_proj, L0_attn_b_proj)
    h = h + _L0_ffn_ref(_layernorm(h, axis=-1), L0_ffn_v_w, L0_ffn_v_b, L0_ffn_gate_w, L0_ffn_gate_b, L0_ffn_w1, L0_ffn_b1, L0_ffn_w2, L0_ffn_b2, L0_ffn_out_w, L0_ffn_out_b, L0_ffn_bk_scale)
    h = h + _L1_attn_ref(_layernorm(h, axis=-1), L1_attn_w_qkv, L1_attn_w_proj, L1_attn_b_proj)
    h = h + _L1_ffn_ref(_layernorm(h, axis=-1), L1_ffn_Wr, L1_ffn_W1, L1_ffn_b1, L1_ffn_W2, L1_ffn_b2)
    return h

_drawn_inputs = setup_inputs


def setup_inputs(seed=0):
    import zlib

    import numpy as np

    out = dict(_drawn_inputs(seed))
    spreads = {'L0_tok_gamma': (1.0, 0.2),
     'L0_tok_beta': (0.0, 0.1),
     'L0_tok_b': (0.0, 0.8),
     'L0_ffn_gate_b': (0.0, 0.8),
     'L0_ffn_b1': (0.0, 0.8),
     'L0_ffn_b2': (0.0, 2.0),
     'L0_ffn_out_b': (0.0, 2.0),
     'L0_ffn_bk_scale': (1.0, 0.6),
     'L1_attn_b_proj': (0.0, 2.0),
     'L1_ffn_b1': (0.0, 0.8),
     'L1_ffn_b2': (0.0, 2.0)}
    factors = {'L0_attn_w_qkv': 5.514,
     'L0_attn_w_proj': 5.551,
     'L0_attn_b_proj': 183.114,
     'L0_ffn_v_w': 200.0,
     'L0_ffn_gate_w': 8.0,
     'L0_ffn_w1': 8.0,
     'L0_ffn_w2': 8.0,
     'L0_ffn_out_w': 64.0,
     'L1_ffn_Wr': 8.0,
     'L1_ffn_W1': 8.0,
     'L1_ffn_W2': 8.0}
    for name, (base, spread) in spreads.items():
        noise = np.random.default_rng([zlib.crc32(name.encode()), seed]).standard_normal(out[name].shape)
        drawn = base * np.exp(spread * noise) if base else spread * noise
        out[name] = jnp.asarray(drawn.astype(out[name].dtype))
    for name, factor in factors.items():
        out[name] = (out[name] * factor).astype(out[name].dtype)
    return out
```

```python
from contextlib import ExitStack

import concourse.bass as bass
from concourse import mybir

F32 = mybir.dt.float32
F32R = mybir.dt.float32r
BF16 = mybir.dt.bfloat16
I32 = mybir.dt.int32
U32 = mybir.dt.uint32
ALU = mybir.AluOpType
ACT = mybir.ActivationFunctionType
AX = mybir.AxisListType

P = 128
S = 32
PATCH, CH, SHIFTS = 16, 3, 5
NPATCH = 36
NTXT = 77
T = NPATCH + NTXT
N = S * T
D = 192
HD = D // 2
HEADS, DH = 12, 16
G, R = 3, 4
E, F = 8, 768
FC = F // P
NF = PATCH * PATCH * SHIFTS * CH
NPIX = PATCH * PATCH * CH + 4 * PATCH * CH
KP = 120
NK = NPIX // KP
NTOK = S * NPATCH // P
TILES = 2 * N // P + E
ROW = 208
EPS_TOK, EPS = 1e-3, 1e-5
V_MAX, FEAT_MAX = 3.0, 10.0
UNUSED = 8192

C_EYE, C_TRI, C_ONE, C_IOTA, C_REV = 0, 128, 256, 384, 512
C_P1 = 640
C_IOT = C_P1 + 1
C_IOB = C_IOT + TILES
C_KEY = C_IOB + S
C_CEIL = C_KEY + E
NCEIL = N // P + 1
C_RST = C_CEIL + NCEIL
C_ALT = C_RST + E * S
C_NHALF = C_ALT + T
C_SEL = C_NHALF + S
C_END = C_SEL + S
FEAT_OPS = 13
CHAIN_PER_TILE = 2
CHAIN_TILES = (T - 1) // CHAIN_PER_TILE


class Idx:

    def __init__(self, m, c, U):
        self.m, self.c, self.U = m, c, U

    def __add__(self, o):
        return Idx(self.m, self.c + o, self.U)

    @property
    def val(self):
        return self.c if isinstance(self.m, int) and self.m == 0 else self.U * self.m + self.c

    @property
    def par(self):
        return self.c % self.U

    @property
    def turn(self):
        q = self.c // self.U
        return q if isinstance(self.m, int) and self.m == 0 else self.m + q

    def live(self, n):
        return not (isinstance(self.m, int) and self.m == 0) or 0 <= self.c < n

    def first(self, n):
        return isinstance(self.m, int) and self.m == 0 and self.c < n


def steps(eng, body, first, last, whole, U):
    lo = -(-whole[0] // U)
    hi = max(lo, (whole[1] + 1) // U)
    for k in range(first, lo * U):
        body(Idx(0, k, U))
    if hi > lo:
        with eng.Fori(lo, hi) as m:
            for u in range(U):
                body(Idx(m, u, U))
    for k in range(hi * U, last + 1):
        body(Idx(0, k, U))


def fusion_kernel(nc, ins, out):
    with ExitStack() as ctx:
        def sb(name, shape, dt=F32):
            return ctx.enter_context(nc.sbuf_tensor(name, shape, dt))

        def dram(name, shape, dt=F32):
            return nc.dram_tensor(name, shape, dt, kind="Internal").ap()

        sems = {}

        def sem(name):
            if name not in sems:
                sems[name] = ctx.enter_context(nc.semaphore(name))
            return sems[name]

        tok_d = dram("tok_d", (S * NPATCH, D))
        rows_d = [dram(f"rows_d{L}", (N, ROW)) for L in range(2)]
        acc_d = [dram("acc_d", (N, D)), out.rearrange("s t d -> (s t) d")]
        feat_d = dram("feat_d", (3, N))

        ps = ctx.enter_context(nc.psum_tensor("ps", [P, 8, 512], F32))
        cst = sb("cst", [P, C_END])
        eye = cst[:, C_EYE:C_EYE + P]
        ones_bf = sb("ones_bf", [P, P], BF16)
        tri_bf = sb("tri_bf", [P, P], BF16)
        w1 = sb("w1", [HD + 1, 2, E * F])
        w2 = sb("w2", [P, E * FC, D])
        b2 = sb("b2", [P, E * D])
        wpr = sb("wpr", [HD, 2, D])
        bpr = sb("bpr", [T, D])
        wg = sb("wg", [HD + 1, 2, E + 1])
        lgt = sb("lgt", [T, S * (E + 1)])
        epst = sb("epst", [P, 2])

        def load(q, dst, src, s, n=16):
            q.dma_start(dst, src).then_inc(sem(s), n)

        UT = 3
        with ExitStack() as early:
            def tb(name, shape, dt=F32):
                return early.enter_context(nc.sbuf_tensor(name, shape, dt))
            wsh = tb("wsh", [KP, SHIFTS, NK, D])
            gam = tb("gam", [KP, 2, SHIFTS, NK])
            weff = tb("weff", [KP, NK, D])
            mult = tb("mult", [P, NPIX])
            pix = [tb(f"pix{i}", [P, NPIX]) for i in range(UT)]
            cen = [tb(f"cen{i}", [P, NPIX]) for i in range(UT)]
            sq = tb("sq", [P, NPIX])
            zT = [tb(f"zT{i}", [KP, NK, P]) for i in range(UT)]
            tmu = [tb(f"tmu{i}", [P, 4]) for i in range(UT)]
            tout = [tb(f"tout{i}", [P, D]) for i in range(UT)]
            brow = tb("brow", [1, D])
            tokb = tb("tokb", [1, D])
            tbias = tb("tbias", [P, D])

        UA = 4
        bst = [sb(f"bst{i}", [T, 6]) for i in range(2)]
        bs2 = [sb(f"bs2{i}", [T, 6]) for i in range(2)]
        mv1 = [sb(f"mv1{i}", [T, 4]) for i in range(2)]
        mv2 = [sb(f"mv2{i}", [T, 4]) for i in range(2)]
        xn = [sb(f"xn{i}", [T, D]) for i in range(2)]
        hb = [sb(f"hb{i}", [T, D]) for i in range(2)]
        h2 = [sb(f"h2{i}", [T, D]) for i in range(UA)]
        x2 = [sb(f"x2{i}", [T, ROW]) for i in range(UA)]
        x2T = [sb(f"x2T{i}", [HD + 1, 2, T]) for i in range(2)]
        psc = sb("psc", [T, D])
        wprb = sb("wprb", [P, G, D], BF16)
        wraw = sb("wraw", [P, G, D])
        avec = sb("avec", [2 * S, T * 2])
        xy = sb("xy", [2 * S, T * 2])
        cur = [sb(f"cur{i}", [2 * S, 2]) for i in range(2)]
        sqj = sb("sqj", [2 * S, 2])
        nrm = sb("nrm", [2 * S, 2])
        gidx = sb("gidx", [P, TILES], U32)
        sidx = sb("sidx", [P, TILES], U32)
        eti = sb("eti", [1, TILES], I32)

        def tb(name, shape, dt=F32):
            return phase.enter_context(nc.sbuf_tensor(name, shape, dt))

        def ab(name, shape, dt=F32):
            return mid.enter_context(nc.sbuf_tensor(name, shape, dt))

        with ExitStack() as phase:
            H = tb("H", [T, S * D])
            wqh = tb("wqh", [P, 2, 2 * G, P], F32R)
            wql = tb("wql", [P, 2, 2 * G, P], F32R)
            wvh = tb("wvh", [P, 2, D], F32R)
            wvl = tb("wvl", [P, 2, D], F32R)
            wqr = tb("wqr", [P, 2, 2 * G, P])
            wvr = tb("wvr", [P, 2, D])
            xTh = [tb(f"xTh{i}", [P, 2, 2, T], F32R) for i in range(2)]
            xTl = [tb(f"xTl{i}", [P, 2, 2, T], F32R) for i in range(2)]
            with ExitStack() as mid:
                qT = [ab(f"qT{i}", [P, G, 2, T]) for i in range(2)]
                kT = [ab(f"kT{i}", [P, G, 2, T]) for i in range(2)]
                vv = [ab(f"vv{i}", [T, HEADS, 2 * DH]) for i in range(2)]
                avT = ab("avT", [P, G * T])
                mx = ab("mx", [T, HEADS])
                pr = ab("pr", [T, R, G, T])
                pT = ab("pT", [T, R, G, T])
                rs = ab("rs", [T, HEADS])
                on = ab("on", [T, HEADS, DH])
                oT = ab("oT", [HD, 2, T])
            with ExitStack() as mid:
                feat = ab("feat", [S, 8, T])
                fT = ab("fT", [3, N])
                spw = ab("spw", [3, D])
                bks = ab("bks", [3, D])
                spg = ab("spg", [3, D])
                waq = ab("waq", [HD, 2, 2 * G * P])
                wav = ab("wav", [HD, 2, D])
                wap = ab("wap", [P, G, D])
            with ExitStack() as mid:
                qTb = [ab(f"qTb{i}", [P, G, 2, T], BF16) for i in range(2)]
                kTb = [ab(f"kTb{i}", [P, G, 2, T], BF16) for i in range(2)]
                vb = [ab(f"vb{i}", [T, HEADS, 2 * DH], BF16) for i in range(2)]
                binq = [ab(f"binq{i}", [T, R, G, T], BF16) for i in range(2)]
                oTb = ab("oTb", [P, G, T], BF16)
                ypr = ab("ypr", [T, D])

        with ExitStack() as phase:
            w1h = tb("w1h", [HD + 1, 2, E * F], F32R)
            with ExitStack() as mid:
                key = ab("key", [T, S, E])
                lg2 = ab("lg2", [T, S, E])
                sel = [ab(f"sel{i}", [T, S, E]) for i in range(2)]
                top = [ab(f"top{i}", [T, S]) for i in range(2)]
                kmx = [ab(f"kmx{i}", [T, S]) for i in range(2)]
                wts = ab("wts", [T, 4, S])
                msk = ab("msk", [T, E, S], BF16)
                incl = ab("incl", [T, E, S])
                pos = ab("pos", [T, E, S])
                ceil = ab("ceil", [T, E, NCEIL])
                cnt = ab("cnt", [T, 4, E])
                slot = ab("slot", [T, 2, S])
                sli = ab("sli", [T, 3, 2 * S], I32)
                hilo = ab("hilo", [T, 2, 2 * S])
                CK = 8
                ohl = [ab(f"ohl{i}", [T, CK, P], BF16) for i in range(2)]
                ohh = ab("ohh", [T, CK, TILES], BF16)
                oht = [ab(f"oht{i}", [T, CK, 2, TILES], BF16) for i in range(2)]
                comb = ab("comb", [T, S, E])
                cmb2 = ab("cmb2", [T, S, E])
                et = ab("et", [1, TILES, E])
                etf = ab("etf", [1, TILES])
                tks = ab("tks", [P, 2, TILES])
                used = ab("used", [P, TILES])
                tid = ab("tid", [P, TILES])
                vcol = ab("vcol", [T, S])
            with ExitStack() as mid:
                UM = 4
                xg = [ab(f"xg{i}", [P, ROW]) for i in range(UM)]
                xgTh = [ab(f"xgTh{i}", [HD + 1, 2, P], F32R) for i in range(UM)]
                xgTl = [ab(f"xgTl{i}", [HD + 1, 2, P], F32R) for i in range(UM)]
                hact = ab("hact", [P, F])
                hTs = ab("hTs", [P, FC, P])
                yb = ab("yb", [P, D])
                yw = [ab(f"yw{i}", [P, D]) for i in range(UM)]
                gcur = [ab(f"gcur{i}", [P, 1], U32) for i in range(UM)]
                scur = [ab(f"scur{i}", [P, 1], U32) for i in range(UM)]

        left = dict.fromkeys("a_h2 a_x2 a_ln a_hb a_bs a_mv a_cs a_nv a_x2T a_xT a_av a_xl a_qm "
                             "a_v a_vc a_pj a_g a_gc a_xc a_oc".split(), S)
        left |= dict.fromkeys("a_mvr a_nvr a_x2c a_qc a_s a_sub".split(), 2 * S)
        left |= dict.fromkeys([f"st_{x}{p}" for x in "hx" for p in range(UA)], 16 * (S // UA))
        left |= dict(a_yp=0, r_gap=1, r_cnt=1, r_exp=1, r_l=2 * S // CK, r_h=3 * (2 * S // CK), r_oh=2 * S // CK)
        left |= dict.fromkeys("m_gi m_si m_yw m_xT m_hT m_hc m_hd m_y m_dn m_xl".split(), TILES)
        left |= dict.fromkeys("m_act m_xc m_up".split(), 2 * TILES) | {"m_sc": 16 * TILES}
        left |= {f"m_g{p}": 16 * len(range(p, TILES, UM)) for p in range(UM)}

        def seen(eng, name, L, count):
            eng.wait_ge(sem(name), count + left[name] if L else count)

        def at(tile, i, n, width=None):
            return tile[:, bass.ds(i.val * n, width or n)]

        nhalf = cst[:, C_NHALF:C_NHALF + 1]
        block = ctx.enter_context(nc.Block())

        TOK = dict(first=-2, last=NTOK - 1, whole=(UT, NTOK - 1 - 2), U=UT)

        def tok_sync(e):
            load(e, cst[:, :], ins["consts"], "consts")
            load(e, gam[:, :, :, :], ins["tok_gb"], "gam_in")
            load(e, tokb[:, :], ins["L0_tok_b"].unsqueeze(0), "gam_in")
            load(e, mult[:, :], ins["mult"], "mult_in")
            for i in range(UT):
                load(e, pix[i][:, :], ins["pixels"][i * P:(i + 1) * P, :], f"pix_in{i}")
            for s in range(SHIFTS):
                load(e, wsh[:, s, :, :], ins["tok_w"][s], f"wsh_in{s}")

            def step(k):
                i = k + 5
                if i.c >= UT and i.live(NTOK):
                    e.wait_ge(sem("tk_cen"), i.val - 2)
                    load(e, pix[i.par][:, :], ins["pixels"][bass.ds(i.val * P, P), :], f"pix_in{i.par}")
                i = k
                if i.live(NTOK):
                    e.wait_ge(sem("tk_out"), i.val + 1)
                    load(e, tok_d[bass.ds(i.val * P, P), :], tout[i.par][:, :], f"tok_st{i.par}")
            steps(e, step, first=-2, last=NTOK - 1, whole=(UT, NTOK - 1 - 5), U=UT)

        def tok_pool(e):
            e.memset(epst[:, 0:1], EPS_TOK).then_inc(sem("eps_set"), 1)
            e.memset(epst[:, 1:2], EPS).then_inc(sem("eps_set"), 1)
            e.wait_ge(sem("consts"), 16)
            e.wait_ge(sem("eps_set"), 2)

            def step(k):
                i = k + 2
                if i.live(NTOK):
                    mu = tmu[i.par]
                    e.wait_ge(sem("tk_var"), i.val + 1)
                    e.tensor_tensor(mu[:, 2:3], mu[:, 1:2], epst[:, 0:1], ALU.add).then_inc(sem("tk_rs"), 1)
                    e.wait_ge(sem("tk_rs"), 2 * i.val + 1)
                    e.tensor_tensor(mu[:, 3:4], mu[:, 2:3], nhalf, ALU.pow).then_inc(sem("tk_rs"), 1)
            steps(e, step, **TOK)

        def tok_vector(e):
            e.wait_ge(sem("consts"), 16)
            e.tensor_copy(ones_bf[:, :], cst[:, C_ONE:C_ONE + P]).then_inc(sem("masks"), 1)
            e.tensor_copy(tri_bf[:, :], cst[:, C_TRI:C_TRI + P]).then_inc(sem("masks"), 1)

            def weights():
                e.wait_ge(sem("gam_in"), 32)
                for s in range(SHIFTS):
                    e.wait_ge(sem(f"wsh_in{s}"), 16)
                    for k in range(NK):
                        if s == 0:
                            e.tensor_scalar(weff[:, k, :], wsh[:, s, k, :], gam[:, 0, s, k:k + 1], None,
                                            ALU.mult).then_inc(sem("weff"), 1)
                        else:
                            e.wait_ge(sem("weff"), (s - 1) * NK + k + 1)
                            e.scalar_tensor_tensor(out=weff[:, k, :], in0=wsh[:, s, k, :],
                                                   scalar=gam[:, 0, s, k:k + 1], in1=weff[:, k, :],
                                                   op0=ALU.mult, op1=ALU.add).then_inc(sem("weff"), 1)
                e.wait_ge(sem("beta_w"), 1)
                e.tensor_tensor(brow[:, :], ps[0:1, 7, 0:D], tokb[:, :], ALU.add).then_inc(sem("brow"), 1)
                e.wait_ge(sem("beta_b"), 1)
                e.tensor_copy(tbias[:, :], ps[:, 7, 0:D]).then_inc(sem("tbias"), 1)

            def centre(i):
                mu = tmu[i.par]
                e.wait_ge(sem(f"pix_in{i.par}"), 16 * (i.turn + 1))
                if not i.first(UT):
                    e.wait_ge(sem("tk_T"), i.val - 2)
                e.tensor_tensor_reduce(cen[i.par][:, :], pix[i.par][:, :], mult[:, :], 1.0 / NF, 0.0,
                                       ALU.mult, ALU.add, mu[:, 0:1]).then_inc(sem("tk_mu"), 1)
                e.wait_ge(sem("tk_mu"), i.val + 1)
                e.tensor_scalar(cen[i.par][:, :], pix[i.par][:, :], mu[:, 0:1], None,
                                ALU.subtract).then_inc(sem("tk_cen"), 1)

            def step(k):
                i = k + 2
                if i.live(NTOK):
                    if i.first(1):
                        e.wait_ge(sem("mult_in"), 16)
                    centre(i)
                i = k + 1
                if i.live(NTOK):
                    e.wait_ge(sem("tk_T"), i.val + 1)
                    if not i.first(2):
                        e.wait_ge(sem("tk_mm"), i.val - 1)
                    e.tensor_copy(zT[i.par][:, NK // 2:, :],
                                  ps[0:KP, 2 * i.par + 1, :].rearrange("p (k t) -> p k t", t=P)
                                  ).then_inc(sem("tk_zd"), 1)
                i = k + 2
                if i.live(NTOK):
                    e.wait_ge(sem("tk_sq"), i.val + 1)
                    e.tensor_tensor_reduce(sq[:, :], sq[:, :], mult[:, :], 1.0 / NF, 0.0,
                                           ALU.mult, ALU.add, tmu[i.par][:, 1:2]).then_inc(sem("tk_var"), 1)
                i = k
                if i.live(NTOK):
                    if i.first(1):
                        weights()
                        e.wait_ge(sem("tbias"), 1)
                    e.wait_ge(sem("tk_mm"), i.val + 1)
                    e.wait_ge(sem("tk_rs"), 2 * i.val + 2)
                    if not i.first(UT):
                        e.wait_ge(sem(f"tok_st{i.par}"), 16 * i.turn)
                    e.scalar_tensor_tensor(out=tout[i.par][:, :], in0=ps[:, 6, 0:D], scalar=tmu[i.par][:, 3:4],
                                           in1=tbias[:, :], op0=ALU.mult, op1=ALU.add).then_inc(sem("tk_out"), 1)
            steps(e, step, **TOK)

        def tok_scalar(e):
            def step(k):
                i = k + 2
                if i.live(NTOK):
                    e.wait_ge(sem("tk_cen"), i.val + 1)
                    if not i.first(1):
                        e.wait_ge(sem("tk_var"), i.val)
                    e.activation(sq[:, :], cen[i.par][:, :], ACT.Square).then_inc(sem("tk_sq"), 1)
                i = k + 1
                if i.live(NTOK):
                    e.wait_ge(sem("tk_T"), i.val + 1)
                    if not i.first(2):
                        e.wait_ge(sem("tk_mm"), i.val - 1)
                    e.copy(zT[i.par][:, 0:NK // 2, :],
                           ps[0:KP, 2 * i.par, :].rearrange("p (k t) -> p k t", t=P)).then_inc(sem("tk_za"), 1)
            steps(e, step, **TOK)

        def tok_tensor(e):
            e.wait_ge(sem("consts"), 16)

            def beta():
                e.wait_ge(sem("gam_in"), 32)
                for s in range(SHIFTS):
                    e.wait_ge(sem(f"wsh_in{s}"), 16)
                    for k in range(NK):
                        mm = e.matmul(ps[0:1, 7, 0:D], gam[:, 1, s, k:k + 1], wsh[:, s, k, :],
                                      start=(s == 0 and k == 0), stop=(s == SHIFTS - 1 and k == NK - 1))
                mm.then_inc(sem("beta_w"), 1)
                e.wait_ge(sem("brow"), 1)
                e.matmul(ps[:, 7, 0:D], cst[0:1, C_ONE:C_ONE + P], brow[:, :],
                         start=True, stop=True).then_inc(sem("beta_b"), 1)

            def step(k):
                i = k + 1
                if i.live(NTOK):
                    e.wait_ge(sem("tk_cen"), i.val + 1)
                    if not i.first(2):
                        e.wait_ge(sem("tk_za"), i.val - 1)
                        e.wait_ge(sem("tk_zd"), i.val - 1)
                    for c in range(NK):
                        mm = e.transpose(ps[0:KP, 2 * i.par + c // 4, (c % 4) * P:(c % 4 + 1) * P],
                                         cen[i.par][:, c * KP:(c + 1) * KP], eye)
                    mm.then_inc(sem("tk_T"), 1)
                i = k
                if i.live(NTOK):
                    if i.first(1):
                        beta()
                        e.wait_ge(sem("weff"), SHIFTS * NK)
                    else:
                        e.wait_ge(sem("tk_out"), i.val)
                    e.wait_ge(sem("tk_za"), i.val + 1)
                    e.wait_ge(sem("tk_zd"), i.val + 1)
                    for c in range(NK):
                        mm = e.matmul(ps[:, 6, 0:D], zT[i.par][:, c, :], weff[:, c, :],
                                      start=(c == 0), stop=(c == NK - 1))
                    mm.then_inc(sem("tk_mm"), 1)
            steps(e, step, **TOK)

        ATT = dict(first=-6, last=S, whole=(4, S - 7), U=UA)

        HALVES = (slice(0, R // 2), slice(R // 2, R))

        def att_sync(e, L):
            if L == 0:
                e.wait_ge(sem("tk_out"), NTOK)
                for p in range(UT):
                    e.wait_ge(sem(f"tok_st{p}"), 16 * (NTOK // UT))
                e.wait_ge(sem("tk_mm"), NTOK)
                Hv = H[:, :].rearrange("t (s d) -> t s d", d=D)
                load(e, Hv[0:NPATCH], tok_d.rearrange("(s t) d -> t s d", t=NPATCH), "h_in0")
                load(e, Hv[NPATCH:T], ins["txt"].rearrange("s t d -> t s d"), "h_in0")
                load(e, wqr[:, :, :, :], ins["wqk0"], "w_in0")
                load(e, wvr[:, :, :], ins["wv0"], "w_in0")
                load(e, wpr[:, :, :], ins["wpr0"], "w_in0")
                load(e, bpr[:, :], ins["bpr0"], "w_in0")
                load(e, wg[:, :, :], ins["wg0"], "w_in0")
            else:
                e.wait_ge(sem("m_sc"), 16 * TILES)
                Hv = H[:, :].rearrange("t (s d) -> t s d", d=D)
                load(e, Hv, acc_d[0].rearrange("(s t) d -> t s d", t=T), "h_in1")
                load(e, wqr[:, :, :, :], ins["wqk1"], "w_in1")
                load(e, wvr[:, :, :], ins["wv1"], "w_in1")
                load(e, wraw[:, :, :], ins["wpr1"], "w_in1")
                load(e, bpr[:, :], ins["bpr1"], "w_in1")
                load(e, wg[:, :, :], ins["wg1"], "w_in1")
                load(e, spw[:, :], ins["spec_w"], "sp_in")
                load(e, bks[:, :], ins["spec_s"], "sp_in")
                e.wait_ge(sem("feats"), FEAT_OPS)
                load(e, feat_d.rearrange("c (s t) -> s c t", t=T), feat[:, 5:8, :], "feat_st")
                e.wait_ge(sem("feat_st"), 16)
                load(e, fT[:, :], feat_d, "feat_in")
            load(e, w1[:, :, :], ins[f"w1_{L}"], f"we_in{L}")
            load(e, w2[:, :, :], ins[f"w2_{L}"], f"we_in{L}")
            load(e, b2[:, :], ins[f"b2_{L}"], f"we_in{L}")

            def step(k):
                i = k
                if i.live(S):
                    seen(e, "a_h2", L, i.val + 1)
                    load(e, acc_d[L][bass.ds(i.val * T, T), :], h2[i.par][:, :], f"st_h{i.par}")
                i = k + -1
                if i.live(S):
                    seen(e, "a_x2", L, i.val + 1)
                    load(e, rows_d[L][bass.ds(i.val * T, T), :], x2[i.par][:, :], f"st_x{i.par}")
            steps(e, step, **ATT)

        def att_pool(e, L):
            if L == 0:
                e.wait_ge(sem("tk_out"), NTOK)
                e.wait_ge(sem("tk_mm"), NTOK)
                for q in range(UT):
                    e.wait_ge(sem(f"tok_st{q}"), 16 * (NTOK // UT))
                for p in range(UA):
                    e.memset(x2[p][:, D:ROW], 0.0).then_inc(sem("x2_set"), 1)
                for p in range(2):
                    e.memset(vv[p][:, :, :], 1.0).then_inc(sem("v_set"), 1)
                e.wait_ge(sem("x2_set"), UA)
                for p in range(UA):
                    e.memset(x2[p][:, D:D + 1], 1.0).then_inc(sem("x2_set"), 1)
            else:
                e.wait_ge(sem("sp_mm"), S // 2)
                for p in range(2):
                    e.memset(vb[p][:, :, :], 0.0).then_inc(sem("vb_set"), 1)
            e.wait_ge(sem(f"w_in{L}"), 80)

            def rstd(m, mv, i):
                seen(e, m, L, i.val + 1)
                e.tensor_tensor(mv[0:T, 2:3], mv[0:T, 1:2], epst[0:T, 1:2], ALU.add).then_inc(sem(m + "r"), 1)
                seen(e, m + "r", L, 2 * i.val + 1)
                e.tensor_tensor(mv[0:T, 3:4], mv[0:T, 2:3], nhalf[0:T], ALU.pow).then_inc(sem(m + "r"), 1)

            def step(k):
                i = k + 6
                if i.live(S):
                    rstd("a_mv", mv1[i.par % 2], i)
                i = k + 1
                if i.live(S):
                    seen(e, "a_ln", L, i.val + 1)
                    if not i.first(2):
                        seen(e, "a_h2", L, i.val - 1)
                    e.tensor_tensor(hb[i.par % 2][:, :], at(H, i, D), bpr[:, :], ALU.add).then_inc(sem("a_hb"), 1)
                i = k
                if i.live(S):
                    rstd("a_nv", mv2[i.par % 2], i)
            steps(e, step, **ATT)

        def part_view(b):
            return (ps[:, 4, 0:4 * T] if b == 4 else ps[:, 5, 0:2 * T]).rearrange("p (g i t) -> p g i t", i=2, t=T)

        def qk_tile(L, j):
            if L == 0:
                return (qT, kT)[j.c % 2][j.c // 2 % 2]
            return (qTb, kTb)[j.c % 2][j.c // 2 % 2]

        def att_vector(e, L):
            if L == 0:
                e.wait_ge(sem("x2_set"), 2 * UA)
                e.wait_ge(sem("v_set"), 2)
                e.wait_ge(sem("wh"), 2)
                e.tensor_tensor(wql[:, :, :, :], wqr[:, :, :, :], wqh[:, :, :, :], ALU.subtract).then_inc(sem("wl"), 1)
                e.tensor_tensor(wvl[:, :, :], wvr[:, :, :], wvh[:, :, :], ALU.subtract).then_inc(sem("wl"), 1)
            else:
                prepare_vector(e)
            for p in range(2):
                e.memset(xTh[p][HD:P, :, :, :].bitcast(F32), 0.0).then_inc(sem("xz"), 1)
                e.memset(xTl[p][HD:P, :, :, :].bitcast(F32), 0.0).then_inc(sem("xz"), 1)
            e.wait_ge(sem(f"h_in{L}"), 32 if L == 0 else 16)

            def residual(k):
                i = k
                if i.live(S):
                    seen(e, "a_pj", L, i.val + 1)
                    seen(e, "a_hb", L, i.val + 1)
                    if not i.first(UA):
                        seen(e, f"st_h{i.par}", L, 16 * i.turn)
                    y = ps[0:T, 6, 0:D]
                    if L == 1:
                        e.tensor_tensor(ypr[:, :], y, psc[:, :], ALU.mult).then_inc(sem("a_yp"), 1)
                        seen(e, "a_yp", L, i.val + 1)
                        y = ypr[:, :]
                    e.tensor_tensor(h2[i.par][:, :], y, hb[i.par % 2][:, :], ALU.add).then_inc(sem("a_h2"), 1)
                    seen(e, "a_h2", L, i.val + 1)
                    e.bn_stats(bs2[i.par % 2][:, :], h2[i.par][:, :]).then_inc(sem("a_cs"), 1)
                    seen(e, "a_cs", L, i.val + 1)

            def step(k):
                i = k + 5
                if i.live(S):
                    mv = mv1[i.par % 2]
                    seen(e, "a_mvr", L, 2 * i.val + 2)
                    if not i.first(2):
                        seen(e, "a_xT", L, i.val - 1)
                    e.tensor_scalar(xn[i.par % 2][:, :], at(H, i, D), mv[:, 0:1], mv[:, 3:4],
                                    ALU.subtract, ALU.mult).then_inc(sem("a_ln"), 1)
                i = k + 6
                if i.live(S):
                    e.bn_stats(bst[i.par % 2][:, :], at(H, i, D)).then_inc(sem("a_bs"), 1)
                i = k + 1
                if i.live(S) and L == 0:
                    for h, rr in enumerate(HALVES):
                        sc = ps[0:T, rr, 0:G * T].rearrange("n r (g m) -> n r g m", g=G)
                        mx3 = mx[:, :].rearrange("n (r g) -> n r g", r=R)[:, rr, :]
                        seen(e, "a_s", L, 2 * i.val + h + 1)
                        e.tensor_reduce(mx3, sc, AX.X, ALU.max).then_inc(sem("a_mx"), 1)
                        seen(e, "a_mx", L, 2 * i.val + h + 1)
                        e.tensor_tensor(pr[:, rr, :, :], sc, mx3.unsqueeze(3).broadcast_to([T, 2, G, T]),
                                        ALU.subtract).then_inc(sem("a_sub"), 1)
                if i.live(S) and L == 1:
                    for h, rr in enumerate(HALVES):
                        seen(e, "a_s", L, 2 * i.val + h + 1)
                        e.tensor_scalar(binq[i.par % 2][:, rr, :, :], ps[0:T, rr, 0:G * T].rearrange("n r (g m) -> n r g m", g=G),
                                        0.0, None, ALU.is_gt).then_inc(sem("a_sub"), 1)
                i = k + -1
                if i.live(S):
                    mv = mv2[i.par % 2]
                    seen(e, "a_nvr", L, 2 * i.val + 2)
                    if not i.first(UA):
                        seen(e, f"st_x{i.par}", L, 16 * i.turn)
                        seen(e, "a_x2T", L, i.val - 3)
                    e.tensor_scalar(x2[i.par][:, 0:D], h2[i.par][:, :], mv[:, 0:1], mv[:, 3:4],
                                    ALU.subtract, ALU.mult).then_inc(sem("a_x2"), 1)
                if (k + 6).live(S):
                    seen(e, "a_bs", L, k.val + 7)
                i = k + 2
                if i.live(S):
                    seen(e, "a_v", L, i.val + 1)
                    if not i.first(2):
                        seen(e, "a_av", L, i.val - 1)
                    src = ps[0:T, 7, 0:D].rearrange("n (h d) -> n h d", h=HEADS)
                    if L == 0:
                        e.tensor_copy(vv[i.par % 2][:, :, 0:DH], src).then_inc(sem("a_vc"), 1)
                    else:
                        e.tensor_scalar(vb[i.par % 2][:, :, 0:DH], src, 0.0, 0.5,
                                        ALU.is_ge, ALU.subtract).then_inc(sem("a_vc"), 1)
                i = k + 6
                if i.live(S):
                    e.bn_aggr(mv1[i.par % 2][:, 0:2], bst[i.par % 2][:, :]).then_inc(sem("a_mv"), 1)
                if L == 1:
                    residual(k)
                j = k + 3
                if j.live(S) and L == 1:
                    seen(e, "a_qm", L, j.val + 1)
                    if not j.first(UA):
                        seen(e, "a_s", L, 2 * (j.val - 2))
                    for b, gs in ((4, slice(0, 2)), (5, slice(2, 3))):
                        e.tensor_scalar(qk_tile(L, j)[:, gs, :, :], part_view(b), 0.0, 0.5,
                                        ALU.is_ge, ALU.subtract).then_inc(sem("a_qc"), 1)
                if L == 1 and k.live(S):
                    e.bn_aggr(mv2[k.par % 2][:, 0:2], bs2[k.par % 2][:, :]).then_inc(sem("a_nv"), 1)
                i = k
                if i.live(S) and L == 0:
                    av = ps[0:T, 6, 0:G * P].rearrange("n (h d) -> n h d", h=HEADS)
                    seen(e, "a_aT", L, i.val + 1)
                    e.reciprocal(rs[:, :], av[:, :, DH]).then_inc(sem("a_rc"), 1)
                    seen(e, "a_rc", L, i.val + 1)
                    if not i.first(1):
                        seen(e, "a_oT", L, i.val)
                    e.tensor_tensor(on[:, :, :], av[:, :, 0:DH], rs[:, :].unsqueeze(2).broadcast_to([T, HEADS, DH]),
                                    ALU.mult).then_inc(sem("a_on"), 1)
                i = k + 1
                if i.live(S) and L == 0:
                    seen(e, "a_pt", L, 2 * i.val + 2)
                    e.tensor_copy(pT[:, 2:4, :, :], ps[0:T, 2:4, 0:G * T].rearrange("m r (g n) -> m r g n", g=G)
                                  ).then_inc(sem("a_pd"), 1)
                i = k + 5
                if i.live(S):
                    seen(e, "a_xc", L, i.val + 1)
                    pb = i.c // 2 % 2
                    e.tensor_tensor(xTl[pb][0:HD, :, i.c % 2, :], ps[0:HD, 4, 0:2 * T].rearrange("p (c t) -> p c t", c=2),
                                    xTh[pb][0:HD, :, i.c % 2, :], ALU.subtract).then_inc(sem("a_xl"), 1)
                if L == 0:
                    residual(k)
                i = k + -1
                if i.live(S):
                    seen(e, "a_g", L, i.val + 1)
                    e.tensor_copy(at(lgt, i, E + 1), ps[0:T, 7, 0:E + 1]).then_inc(sem("a_gc"), 1)
                if L == 0 and k.live(S):
                    e.bn_aggr(mv2[k.par % 2][:, 0:2], bs2[k.par % 2][:, :]).then_inc(sem("a_nv"), 1)
            steps(e, step, **ATT)

        def att_scalar(e, L):
            if L == 0:
                e.wait_ge(sem("w_in0"), 80)
                e.copy(wqh[:, :, :, :], wqr[:, :, :, :]).then_inc(sem("wh"), 1)
                e.copy(wvh[:, :, :], wvr[:, :, :]).then_inc(sem("wh"), 1)
            else:
                prepare_scalar(e)

            def step(k):
                def exp(h):
                    i = k + 1
                    if i.live(S) and L == 0:
                        seen(e, "a_sub", L, 2 * i.val + h + 1)
                        e.activation(pr[:, HALVES[h], :, :], pr[:, HALVES[h], :, :], ACT.Exp).then_inc(sem("a_e"), 1)
                exp(0)
                i = k
                if i.live(S):
                    seen(e, "a_av", L, i.val + 1)
                    if L == 0:
                        if not i.first(1):
                            seen(e, "a_aT", L, i.val)
                        e.copy(avT[:, :], ps[:, 6, 0:G * T]).then_inc(sem("a_ac"), 1)
                    else:
                        if not i.first(1):
                            seen(e, "a_pj", L, i.val)
                        e.copy(oTb[:, :, :], ps[:, 6, 0:G * T].rearrange("p (g t) -> p g t", g=G)
                               ).then_inc(sem("a_oc"), 1)
                exp(1)
                i = k + 1
                if i.live(S) and L == 0:
                    seen(e, "a_pt", L, 2 * i.val + 1)
                    e.copy(pT[:, 0:2, :, :], ps[0:T, 0:2, 0:G * T].rearrange("m r (g n) -> m r g n", g=G)
                           ).then_inc(sem("a_pa"), 1)
                j = k + 3
                if j.live(S) and L == 0:
                    seen(e, "a_qm", L, j.val + 1)
                    if not j.first(UA):
                        seen(e, "a_s", L, 2 * (j.val - 2))
                    scale = 1.0 if j.c % 2 else DH ** -0.5
                    for b, gs in ((4, slice(0, 2)), (5, slice(2, 3))):
                        e.mul(qk_tile(L, j)[:, gs, :, :], part_view(b), scale).then_inc(sem("a_qc"), 1)
                i = k + -1
                if i.live(S):
                    seen(e, "a_x2T", L, i.val + 1)
                    if not i.first(2):
                        seen(e, "a_g", L, i.val - 1)
                    src = ps[:, 7, 0:2 * T].rearrange("p (c t) -> p c t", c=2)
                    e.copy(x2T[i.par % 2][0:HD, 0, :], src[0:HD, 0, :]).then_inc(sem("a_x2c"), 1)
                    e.copy(x2T[i.par % 2][:, 1, :], src[0:HD + 1, 1, :]).then_inc(sem("a_x2c"), 1)
                i = k + 5
                if i.live(S):
                    seen(e, "a_xT", L, i.val + 1)
                    if not i.first(UA):
                        seen(e, "a_v", L, i.val - 2)
                    e.copy(xTh[i.c // 2 % 2][0:HD, :, i.c % 2, :], ps[0:HD, 4, 0:2 * T].rearrange("p (c t) -> p c t", c=2)
                           ).then_inc(sem("a_xc"), 1)
                i = k
                if i.live(S) and L == 0:
                    seen(e, "a_oT", L, i.val + 1)
                    if not i.first(1):
                        seen(e, "a_pj", L, i.val)
                    e.copy(oT[:, :, :], ps[0:HD, 6, 0:2 * T].rearrange("p (c t) -> p c t", c=2)).then_inc(sem("a_oc"), 1)
            steps(e, step, **ATT)

        def att_tensor(e, L):
            if L == 0:
                e.wait_ge(sem("wl"), 2)
            else:
                prepare_tensor(e)
                e.wait_ge(sem("signs"), 5)
            e.wait_ge(sem(f"w_in{L}"), 80)
            dh = 32 if L == 0 else DH
            e.wait_ge(sem("xz"), 4 * (L + 1))
            passes = ((0, 0), (0, 1), (1, 0)) if L == 0 else ((0, 0), (0, 1))
            wq_, wv_, x_ = (wqh, wql), (wvh, wvl), (xTh, xTl)

            def turn(k, h):
                i = k + 1
                if i.live(S) and L == 0:
                    seen(e, "a_e", L, 2 * i.val + h + 1)
                    for r in range(HALVES[h].start, HALVES[h].stop):
                        for g in range(G):
                            mm = e.transpose(ps[0:T, r, g * T:(g + 1) * T], pr[:, r, g, :], eye[0:T, 0:T])
                    mm.then_inc(sem("a_pt"), 1)

            def project(k):
                i = k
                if i.live(S):
                    seen(e, "a_oc", L, i.val + 1)
                    if L == 0:
                        for c in range(2):
                            mm = e.matmul(ps[0:T, 6, 0:D], oT[:, c, :], wpr[:, c, :], start=(c == 0), stop=(c == 1))
                    else:
                        for g in range(G):
                            mm = e.matmul(ps[0:T, 6, 0:D], oTb[:, g, :], wprb[:, g, :],
                                          start=(g == 0), stop=(g == G - 1))
                    mm.then_inc(sem("a_pj"), 1)

            def step(k):
                i = k + 1
                if i.live(S):
                    seen(e, "a_qc", L, 2 * (i.val + 2 - i.c % 2))
                    pb, u = i.c // 2 % 2, i.c % 2
                    q_, k_ = (qT[pb], kT[pb]) if L == 0 else (kTb[pb], qTb[pb])
                    for h, rr in enumerate(HALVES):
                        if not i.first(1):
                            if L == 0:
                                seen(e, ("a_pa", "a_pd")[h], L, i.val)
                            else:
                                seen(e, "a_sub", L, 2 * i.val + h - 1)
                        for g in range(G):
                            for r in range(rr.start, rr.stop):
                                mm = e.matmul(ps[0:T, r, g * T:(g + 1) * T], q_[32 * r:32 * r + dh, g, u, :],
                                              k_[32 * r:32 * r + dh, g, u, :], start=True, stop=True)
                        mm.then_inc(sem("a_s"), 1)
                i = k
                if i.live(S):
                    seen(e, "a_vc", L, i.val + 1)
                    if not i.first(1):
                        seen(e, "a_h2" if L == 0 else "a_yp", L, i.val)
                    if L == 0:
                        seen(e, "a_pa", L, i.val + 1)
                        seen(e, "a_pd", L, i.val + 1)
                    else:
                        seen(e, "a_sub", L, 2 * i.val + 2)
                    for g in range(G):
                        for r in range(R):
                            v_ = vv[i.par % 2] if L == 0 else vb[i.par % 2]
                            w_ = pT[:, r, g, :] if L == 0 else binq[i.par % 2][:, r, g, :]
                            mm = e.matmul(ps[32 * r:32 * r + 32, 6, g * T:(g + 1) * T], v_[:, R * g + r, :], w_,
                                          start=True, stop=True)
                    mm.then_inc(sem("a_av"), 1)
                i = k + 2
                if i.live(S):
                    seen(e, "a_xl", L, i.val + 1)
                    if (k + -2).live(S):
                        seen(e, "a_gc", L, k.val - 1)
                    elif not i.first(1):
                        seen(e, "a_vc", L, i.val)
                    n_ = 2 * len(passes)
                    for c in range(2):
                        for a, b in passes:
                            n_ -= 1
                            mm = e.matmul(ps[0:T, 7, 0:D], x_[b][i.c // 2 % 2][:, c, i.c % 2, :], wv_[a][:, c, :],
                                          start=(n_ == 2 * len(passes) - 1), stop=(n_ == 0))
                    mm.then_inc(sem("a_v"), 1)
                turn(k, 0)
                if L == 1:
                    project(k)
                i = k
                if i.live(S) and L == 0:
                    seen(e, "a_ac", L, i.val + 1)
                    for g in range(G):
                        mm = e.transpose(ps[0:T, 6, g * P:(g + 1) * P], avT[:, g * T:(g + 1) * T], eye)
                    mm.then_inc(sem("a_aT"), 1)
                j = k + 3
                if j.live(S):
                    p = j.c // 2 * 2 - j.c
                    seen(e, "a_xl", L, j.val + p + 2)
                    if (k + 4).live(S):
                        seen(e, "a_xl", L, k.val + 5)
                    for g in range(G):
                        n_ = 0
                        for c in range(2):
                            for a, b in passes:
                                mm = e.matmul(ps[:, 4 + g // 2, g % 2 * 2 * T:(g % 2 + 1) * 2 * T],
                                              wq_[a][:, c, G * (j.c % 2) + g, :],
                                              x_[b][j.c // 2 % 2][:, c, :, :].rearrange("p i t -> p (i t)"),
                                              start=(n_ == 0), stop=(n_ == 2 * len(passes) - 1))
                                n_ += 1
                    mm.then_inc(sem("a_qm"), 1)
                turn(k, 1)
                i = k + -1
                if i.live(S):
                    seen(e, "a_x2", L, i.val + 1)
                    if (k + 2).live(S):
                        seen(e, "a_vc", L, k.val + 3)
                    e.transpose(ps[0:HD, 7, 0:T], x2[i.par][:, 0:HD], eye[0:T, 0:T])
                    e.transpose(ps[0:HD + 1, 7, T:2 * T], x2[i.par][:, HD:D + 1],
                                eye[0:T, 0:T]).then_inc(sem("a_x2T"), 1)
                i = k + 5
                if i.live(S):
                    seen(e, "a_ln", L, i.val + 1)
                    if (k + 3).live(S):
                        seen(e, "a_qc", L, 2 * (k.val + 4))
                    elif not i.first(1):
                        seen(e, "a_xl", L, i.val)
                    e.transpose(ps[0:HD, 4, 0:T], xn[i.par % 2][:, 0:HD], eye[0:T, 0:T])
                    e.transpose(ps[0:HD, 4, T:2 * T], xn[i.par % 2][:, HD:D], eye[0:T, 0:T]).then_inc(sem("a_xT"), 1)
                i = k
                if i.live(S) and L == 0:
                    seen(e, "a_on", L, i.val + 1)
                    o = on[:, :, :].rearrange("n h d -> n (h d)")
                    e.transpose(ps[0:HD, 6, 0:T], o[:, 0:HD], eye[0:T, 0:T])
                    e.transpose(ps[0:HD, 6, T:2 * T], o[:, HD:D], eye[0:T, 0:T]).then_inc(sem("a_oT"), 1)
                i = k + -1
                if i.live(S):
                    seen(e, "a_x2c", L, 2 * i.val + 2)
                    for c in range(2):
                        kk = HD + c
                        mm = e.matmul(ps[0:T, 7, 0:E + 1], x2T[i.par % 2][0:kk, c, :], wg[0:kk, c, :],
                                      start=(c == 0), stop=(c == 1))
                    mm.then_inc(sem("a_g"), 1)
                if L == 0:
                    project(k)
            steps(e, step, **ATT)

        def prepare_scalar(e):
            e.wait_ge(sem("w_in1"), 80)
            e.activation(waq[:, :, :], wqr[0:HD, :, :, :].rearrange("p c j o -> p c (j o)"), ACT.Abs).then_inc(sem("wabs"), 1)
            e.activation(wav[:, :, :], wvr[0:HD, :, :], ACT.Abs).then_inc(sem("wabs"), 1)
            e.activation(wap[:, :, :], wraw[:, :, :], ACT.Abs).then_inc(sem("wabs"), 1)

        def prepare_tensor(e):
            half_w = G * P
            e.wait_ge(sem("wabs"), 3)
            for b in range(2):
                for c in range(2):
                    e.matmul(ps[:, b, 0:half_w], cst[0:HD, C_ONE:C_ONE + P],
                             waq[:, c, b * half_w:(b + 1) * half_w], start=(c == 0), stop=(c == 1))
            for c in range(2):
                e.matmul(ps[:, 2, 0:D], cst[0:HD, C_ONE:C_ONE + P], wav[:, c, :], start=(c == 0), stop=(c == 1))
            for g in range(G):
                mm = e.matmul(ps[0:T, 3, 0:D], cst[:, C_ONE:C_ONE + T], wap[:, g, :], start=(g == 0), stop=(g == G - 1))
            mm.then_inc(sem("abs_sum"), 1)
            e.wait_ge(sem("chain"), 4 * (T - 1) + 3)
            e.matmul(ps[0:S, 6, 0:2 * T], cst[0:2 * S, C_SEL:C_SEL + S], xy[:, :], start=True,
                     stop=True).then_inc(sem("chain_b"), 1)
            e.wait_ge(sem("feat_in"), 16)
            e.wait_ge(sem("spg"), 1)
            for i in range(S):
                if i % 2 == 0 and i >= 4:
                    e.wait_ge(sem("sp_add"), i // 2 - 1)
                mm = e.matmul(ps[0:T, 4 + i // 2 % 2, (i % 2) * D:(i % 2 + 1) * D], fT[:, i * T:(i + 1) * T],
                              spg[:, :], start=True, stop=True)
                if i % 2:
                    mm.then_inc(sem("sp_mm"), 1)

        def prepare_vector(e):
            seq = [0]

            def chained(ins_):
                seq[0] += 1
                ins_.then_inc(sem("feats"), 1)
                e.wait_ge(sem("feats"), seq[0])

            fw = xy[0:S, :].rearrange("s (t c) -> s t c", c=2)
            av = avec[0:S, :].rearrange("s (t c) -> s t c", c=2)
            bw = ps[0:S, 6, 0:2 * T].rearrange("s (t c) -> s t c", c=2)
            alt = cst[0:S, C_ALT:C_ALT + T]
            e.wait_ge(sem("chain_b"), 1)
            f = [feat[:, j, :] for j in range(8)]
            chained(e.tensor_tensor(f[0], fw[:, :, 0], bw[:, ::-1, 0], ALU.add))
            chained(e.tensor_tensor(f[0], f[0], av[:, :, 0], ALU.subtract))
            chained(e.tensor_tensor(f[0], f[0], alt, ALU.mult))
            chained(e.tensor_tensor(f[1], fw[:, :, 1], bw[:, ::-1, 1], ALU.add))
            chained(e.tensor_tensor(f[1], f[1], av[:, :, 1], ALU.subtract))
            chained(e.tensor_tensor(f[2], f[0], f[0], ALU.mult))
            chained(e.tensor_tensor(f[3], f[1], f[1], ALU.mult))
            chained(e.tensor_tensor(f[2], f[2], f[3], ALU.add))
            chained(e.reciprocal(f[4], f[2]))
            chained(e.tensor_tensor(f[5], f[0], f[4], ALU.mult))
            chained(e.scalar_tensor_tensor(out=f[6], in0=f[1], scalar=-1.0, in1=f[4], op0=ALU.mult, op1=ALU.mult))
            chained(e.tensor_scalar(feat[:, 5:7, :], feat[:, 5:7, :], FEAT_MAX, -FEAT_MAX, ALU.min, ALU.max))
            e.memset(f[7], 1.0).then_inc(sem("feats"), 1)
            e.wait_ge(sem("abs_sum"), 1)
            e.tensor_scalar(wqr[:, :, :, :], wqr[:, :, :, :], 0.0, 0.5, ALU.is_ge, ALU.subtract).then_inc(sem("signs0"), 1)
            e.tensor_scalar(wvr[:, :, :], wvr[:, :, :], 0.0, 0.5, ALU.is_ge, ALU.subtract).then_inc(sem("signs0"), 1)
            e.wait_ge(sem("signs0"), 2)
            for c in range(2):
                two = lambda w: w[:, c, :, :].rearrange("p (b j) o -> p b (j o)", b=2)
                e.scalar_tensor_tensor(out=two(wqh), in0=ps[:, 0:2, 0:G * P], scalar=0.0, in1=two(wqr),
                                       op0=ALU.is_gt, op1=ALU.mult).then_inc(sem("signs"), 1)
                e.scalar_tensor_tensor(out=wvh[:, c, :], in0=ps[:, 2, 0:D], scalar=0.0, in1=wvr[:, c, :],
                                       op0=ALU.is_gt, op1=ALU.mult).then_inc(sem("signs"), 1)
            e.tensor_scalar(wprb[:, :, :], wraw[:, :, :], 0.0, 0.5, ALU.is_ge, ALU.subtract).then_inc(sem("signs"), 1)
            e.tensor_scalar(psc[:, :], ps[0:T, 3, 0:D], 4.0 / D, None, ALU.mult).then_inc(sem("psc"), 1)
            e.wait_ge(sem("sp_in"), 32)
            e.tensor_tensor(spg[:, :], spw[:, :], bks[:, :], ALU.mult).then_inc(sem("spg"), 1)
            e.wait_ge(sem("h_in1"), 16)
            for j in range(S // 2):
                hj = H[:, 2 * j * D:2 * (j + 1) * D]
                e.wait_ge(sem("sp_mm"), j + 1)
                e.tensor_tensor(hj, hj, ps[0:T, 4 + j % 2, 0:2 * D], ALU.add).then_inc(sem("sp_add"), 1)
            e.wait_ge(sem("sp_add"), S // 2)
            e.wait_ge(sem("psc"), 1)
            e.wait_ge(sem("vb_set"), 2)

        KB = 2 * S

        def route_vector(e, L):
            seq = [0]

            def chained(ins_):
                seq[0] += 1
                ins_.then_inc(sem(f"r_dve{L}"), 1)
                e.wait_ge(sem(f"r_dve{L}"), seq[0])

            def bc(x, axis, shape):
                return x.unsqueeze(axis).broadcast_to(shape)

            TSE, TES = [T, S, E], [T, E, S]
            seen(e, "a_gc", L, S)
            lg = lgt[:, :].rearrange("t (s e) -> t s e", e=E + 1)
            keys = bc(cst[0:T, C_KEY:C_KEY + E], 1, TSE)
            if L == 0:
                chained(e.tensor_scalar(vcol[:, :], lg[:, :, E], V_MAX, -V_MAX, ALU.min, ALU.max))
            chained(e.tensor_copy(lg2[:, :, :], lg[:, :, 0:E]))
            for c in range(2):
                chained(e.tensor_reduce(top[c][:, :], lg2[:, :, :], AX.X, ALU.max))
                chained(e.tensor_tensor(key[:, :, :], lg2[:, :, :], bc(top[c][:, :], 2, TSE), ALU.is_equal))
                chained(e.tensor_tensor(key[:, :, :], key[:, :, :], keys, ALU.mult))
                chained(e.tensor_reduce(kmx[c][:, :], key[:, :, :], AX.X, ALU.max))
                chained(e.tensor_tensor(sel[c][:, :, :], keys, bc(kmx[c][:, :], 2, TSE), ALU.is_equal))
                if c == 0:
                    chained(e.scalar_tensor_tensor(out=lg2[:, :, :], in0=sel[0][:, :, :], scalar=-3e38,
                                                   in1=lg2[:, :, :], op0=ALU.mult, op1=ALU.add))
            chained(e.tensor_tensor(msk[:, :, :].rearrange("t e s -> t s e"), sel[0][:, :, :], sel[1][:, :, :], ALU.add))
            e.tensor_tensor(wts[:, 0, :], top[1][:, :], top[0][:, :], ALU.subtract).then_inc(sem("r_gap"), 1)
            seen(e, "r_cnt", L, 1)
            within = ps[0:T, 0, 0:E * S]
            total = ps[0:T, 1, 0:E * S]
            inc2 = incl[:, :, :].rearrange("t e s -> t (e s)")
            chained(e.tensor_tensor_scan(inc2, cst[0:T, C_RST:C_RST + E * S], total, 0.0, ALU.mult, ALU.add))
            chained(e.tensor_tensor(ceil[:, :, :], bc(incl[:, :, S - 1], 2, [T, E, NCEIL]),
                                    bc(cst[0:T, C_CEIL:C_CEIL + NCEIL], 1, [T, E, NCEIL]), ALU.is_gt))
            chained(e.tensor_reduce(cnt[:, 0, :], ceil[:, :, :], AX.X, ALU.add))
            chained(e.tensor_tensor_scan(cnt[:, 1, :], cst[0:T, C_ONE:C_ONE + E], cnt[:, 0, :], 0.0, ALU.mult, ALU.add))
            chained(e.tensor_tensor(cnt[:, 2, :], cnt[:, 1, :], cnt[:, 0, :], ALU.subtract))
            chained(e.tensor_scalar(cnt[:, 3, :], cnt[:, 2, :], float(P), None, ALU.mult))
            pos2 = pos[:, :, :].rearrange("t e s -> t (e s)")
            chained(e.tensor_tensor(pos2, inc2, total, ALU.subtract))
            chained(e.tensor_tensor(pos2, pos2, within, ALU.add))
            chained(e.tensor_tensor(pos[:, :, :], pos[:, :, :], bc(cnt[:, 3, :], 2, TES), ALU.add))
            for c in range(2):
                chained(e.tensor_tensor(key[:, :, :], sel[c][:, :, :], pos[:, :, :].rearrange("t e s -> t s e"), ALU.mult))
                chained(e.tensor_reduce(slot[:, c, :], key[:, :, :], AX.X, ALU.add))
            chained(e.tensor_copy(sli[:, 0, :], slot[:, :, :].rearrange("t c s -> t (c s)")))
            chained(e.tensor_scalar(sli[:, 1, :], sli[:, 0, :], 7, None, ALU.logical_shift_right))
            chained(e.tensor_scalar(sli[:, 2, :], sli[:, 0, :], P - 1, None, ALU.bitwise_and))
            chained(e.tensor_copy(hilo[:, :, :], sli[:, 1:3, :]))
            chained(e.tensor_tensor(et[:, :, :], bc(cst[0:1, C_IOT:C_IOT + TILES], 2, [1, TILES, E]),
                                    bc(cnt[0:1, 1, :], 1, [1, TILES, E]), ALU.is_ge))
            chained(e.tensor_reduce(etf[:, :], et[:, :, :], AX.X, ALU.add))
            chained(e.tensor_scalar(eti[:, :], etf[:, :], float(E - 1), None, ALU.min))
            seen(e, "r_exp", L, 1)
            chained(e.tensor_scalar(wts[:, 2, :], wts[:, 1, :], 1.0, None, ALU.add))
            chained(e.reciprocal(wts[:, 2, :], wts[:, 2, :]))
            chained(e.tensor_tensor(wts[:, 3, :], wts[:, 1, :], wts[:, 2, :], ALU.mult))
            chained(e.tensor_tensor(comb[:, :, :], sel[0][:, :, :], bc(wts[:, 2, :], 2, TSE), ALU.mult))
            chained(e.tensor_tensor(cmb2[:, :, :], sel[1][:, :, :], bc(wts[:, 3, :], 2, TSE), ALU.mult))
            chained(e.tensor_tensor(comb[:, :, :], comb[:, :, :], cmb2[:, :, :], ALU.add))
            for c in range(KB // CK):
                p = c % 2
                ksl = slice(c * CK, (c + 1) * CK)
                if c >= 2:
                    seen(e, "r_oh", L, c - 1)
                e.tensor_tensor(ohl[p][:, :, :], bc(cst[0:T, C_IOTA:C_IOTA + P], 1, [T, CK, P]),
                                bc(hilo[:, 1, ksl], 2, [T, CK, P]), ALU.is_equal).then_inc(sem("r_l"), 1)
                if c >= 1:
                    seen(e, "r_h", L, 3 * c)
                e.tensor_tensor(ohh[:, :, :], bc(cst[0:T, C_IOT:C_IOT + TILES], 1, [T, CK, TILES]),
                                bc(hilo[:, 0, ksl], 2, [T, CK, TILES]), ALU.is_equal).then_inc(sem("r_h"), 1)
                seen(e, "r_h", L, 3 * c + 1)
                e.tensor_scalar(oht[p][:, :, 0, :], ohh[:, :, :], cst[0:T, C_P1:C_P1 + 1], None,
                                ALU.mult).then_inc(sem("r_h"), 1)
                b0 = C_IOB + (c * CK) % S
                e.tensor_tensor(oht[p][:, :, 1, :], ohh[:, :, :], bc(cst[0:T, b0:b0 + CK], 2, [T, CK, TILES]),
                                ALU.mult).then_inc(sem("r_h"), 1)
            seen(e, "r_oh", L, KB // CK)
            chained(e.tensor_copy(tks[:, :, :], ps[:, 5, 0:2 * TILES].rearrange("p (a j) -> p a j", a=2)))
            chained(e.tensor_scalar(used[:, :], tks[:, 0, :], 1.0, None, ALU.min))
            chained(e.scalar_tensor_tensor(out=tid[:, :], in0=tks[:, 1, :], scalar=float(T), in1=tks[:, 0, :],
                                           op0=ALU.mult, op1=ALU.add))
            chained(e.tensor_tensor(gidx[:, :], tid[:, :], used[:, :], ALU.subtract))
            chained(e.tensor_scalar(used[:, :], used[:, :], -UNUSED - 1.0, float(UNUSED), ALU.mult, ALU.add))
            chained(e.tensor_tensor(sidx[:, :], tid[:, :], used[:, :], ALU.add))
            return seq[0]

        def route_tensor(e, L):
            e.wait_ge(sem("masks"), 2)
            seen(e, "r_gap", L, 1)
            m = msk[:, :, :].rearrange("t e s -> t (e s)")
            e.matmul(ps[0:T, 0, 0:E * S], tri_bf[0:T, 0:T], m, start=True, stop=True)
            e.matmul(ps[0:T, 1, 0:E * S], ones_bf[0:T, 0:T], m, start=True, stop=True).then_inc(sem("r_cnt"), 1)
            if L == 0:
                e.matmul(ps[0:S, 6, 0:T], vcol[:, :], eye[0:T, 0:T], start=True, stop=True)
                e.matmul(ps[S:2 * S, 6, 0:T], vcol[:, :], cst[0:T, C_REV:C_REV + T], start=True,
                         stop=True).then_inc(sem("vrow"), 1)
            for c in range(KB // CK):
                seen(e, "r_l", L, c + 1)
                seen(e, "r_h", L, 3 * c + 3)
                for q in range(CK):
                    j = c * CK + q
                    mm = e.matmul(ps[:, 5, 0:2 * TILES], ohl[c % 2][:, q, :],
                                  oht[c % 2][:, q, :, :].rearrange("t a j -> t (a j)"),
                                  start=(j == 0), stop=(j == KB - 1))
                mm.then_inc(sem("r_oh"), 1)

        def route_scalar(e, L):
            seen(e, "r_gap", L, 1)
            e.activation(wts[:, 1, :], wts[:, 0, :], ACT.Exp).then_inc(sem("r_exp"), 1)

        def route_sync(e, L):
            for p in range(UA):
                seen(e, f"st_x{p}", L, 16 * (S // UA))
            e.wait_ge(sem(f"r_dve{L}"), ROUTE_COMB[L])
            load(e, rows_d[L].rearrange("(s t) c -> t s c", t=T)[:, :, D + 1:D + 1 + E], comb[:, :, :], f"comb{L}")

        EXP = dict(first=-2, last=TILES - 1, whole=(4, TILES - 1 - 4), U=UM)

        def exp_pool(e, L):
            e.wait_ge(sem(f"comb{L}"), 16)
            for p in range(UA):
                seen(e, f"st_h{p}", L, 16 * (S // UA))
            e.wait_ge(sem(f"r_dve{L}"), ROUTE_ALL[L])
            bound = e.to_reg(N - 1)


            def copy_index(cur_, table, count, i):
                e.tensor_copy(cur_[i.par][:, :], at(table, i, 1)).then_inc(sem(count), 1)

            def gather(i):
                e.indirect_dma_start(out=xg[i.par][:, :], out_offset=None, in_=rows_d[L],
                                     in_offset=bass.IndirectOffsetOnAxis(ap=gcur[i.par][:, :], axis=0),
                                     bounds_check=bound, oob_is_err=False).then_inc(sem(f"m_g{i.par}"), 16)

            for c in range(UM):
                copy_index(gcur, gidx, "m_gi", Idx(0, c, UM))
            copy_index(scur, sidx, "m_si", Idx(0, 0, UM))
            for c in range(UM):
                seen(e, "m_gi", L, c + 1)
                gather(Idx(0, c, UM))
            seen(e, "m_g0", L, 16)
            copy_index(gcur, gidx, "m_gi", Idx(0, UM, UM))

            def step(k):
                i = k
                seen(e, "m_si", L, i.val + 1)
                seen(e, "m_yw", L, i.val + 1)
                if not i.first(1):
                    seen(e, "m_sc", L, 16 * i.val)
                if (k + 1).live(TILES):
                    copy_index(scur, sidx, "m_si", k + 1)
                e.indirect_dma_start(out=acc_d[L], out_offset=bass.IndirectOffsetOnAxis(ap=scur[i.par][:, :], axis=0),
                                     in_=yw[i.par][:, :], in_offset=None, bounds_check=bound, oob_is_err=False,
                                     compute_op=ALU.add).then_inc(sem("m_sc"), 16)
                i = k + UM
                if i.live(TILES):
                    seen(e, "m_gi", L, i.val + 1)
                    seen(e, "m_xT", L, k.val + 1)
                    if (i + 1).live(TILES):
                        seen(e, f"m_g{(k + 1).par}", L, 16 * ((k + 1).turn + 1))
                        copy_index(gcur, gidx, "m_gi", i + 1)
                    gather(i)
            steps(e, step, first=0, last=TILES - 1, whole=(4, TILES - 1 - 5), U=UM)
            seen(e, "m_sc", L, 16 * TILES)

        def expert_of(e, i):
            return e.value_load(eti[0:1, bass.ds(i.val, 1)], min_val=0, max_val=E - 1)

        def exp_tensor(e, L):
            e.wait_ge(sem(f"r_dve{L}"), ROUTE_ALL[L])
            e.wait_ge(sem(f"we_in{L}"), 48)
            e.wait_ge(sem("w1_lo"), E * (L + 1))
            w1l = w1[:, :, :].bitcast(F32R)

            def step(k):
                ex_up = expert_of(e, k + 1) if (k + 1).live(TILES) else None
                ex_dn = expert_of(e, k) if k.live(TILES) else None
                i = k
                if i.live(TILES):
                    seen(e, "m_act", L, 2 * i.val + 2)
                    for c in range(FC):
                        mm = e.transpose(ps[:, 2 + c // 3, (c % 3) * P:(c % 3 + 1) * P], hact[:, c * P:(c + 1) * P], eye)
                    mm.then_inc(sem("m_hT"), 1)
                i = k + 2
                if i.live(TILES):
                    seen(e, f"m_g{i.par}", L, 16 * (i.turn + 1))
                    if not i.first(1):
                        seen(e, "m_xl", L, i.val)
                    e.transpose(ps[0:HD, 5, 0:P], xg[i.par][:, 0:HD], eye)
                    e.transpose(ps[0:HD + 1, 5, P:2 * P], xg[i.par][:, HD:D + 1], eye).then_inc(sem("m_xT"), 1)
                i = k + 1
                if i.live(TILES):
                    seen(e, "m_xl", L, i.val + 1)
                    for b in range(2):
                        n_ = 0
                        for x_, w_ in ((xgTh, w1h), (xgTl, w1h), (xgTh, w1l)):
                            for c in range(2):
                                kk = HD + c
                                w = w_[0:kk, c, bass.ds(ex_up * F + b * (F // 2), F // 2)]
                                mm = e.matmul(ps[:, b, 0:F // 2], x_[i.par][0:kk, c, :], w, start=(n_ == 0), stop=(n_ == 5))
                                n_ += 1
                        mm.then_inc(sem("m_up"), 1)
                i = k
                if i.live(TILES):
                    seen(e, "m_hc", L, i.val + 1)
                    seen(e, "m_hd", L, i.val + 1)
                    if not i.first(1):
                        seen(e, "m_y", L, i.val)
                    w2f = w2[:, :, :].rearrange("p c d -> p (c d)")
                    for c in range(FC):
                        mm = e.matmul(ps[:, 4, 0:D], hTs[:, c, :], w2f[:, bass.ds(ex_dn * (FC * D) + c * D, D)],
                                      start=(c == 0), stop=(c == FC - 1))
                    mm.then_inc(sem("m_dn"), 1)
            steps(e, step, **EXP)

        def split_scalar(e, L):
            e.wait_ge(sem(f"we_in{L}"), 48)
            seen(e, "a_gc", L, S)
            for x in range(E):
                e.copy(w1h[:, :, x * F:(x + 1) * F], w1[:, :, x * F:(x + 1) * F]).then_inc(sem("w1_hi"), 1)

        def split_pool(e, L):
            for x in range(E):
                e.wait_ge(sem("w1_hi"), E * L + x + 1)
                w = w1[:, :, x * F:(x + 1) * F]
                e.tensor_tensor(w.bitcast(F32R), w, w1h[:, :, x * F:(x + 1) * F], ALU.subtract).then_inc(sem("w1_lo"), 1)

        def exp_scalar(e, L):
            func = ACT.Gelu_apprx_tanh if L == 0 else ACT.Relu

            def step(k):
                i = k
                if i.live(TILES):
                    seen(e, "m_hT", L, i.val + 1)
                    if not i.first(1):
                        seen(e, "m_dn", L, i.val)
                    e.copy(hTs[:, 0:3, :], ps[:, 2, 0:3 * P].rearrange("p (c t) -> p c t", c=3)).then_inc(sem("m_hc"), 1)
                i = k + 2
                if i.live(TILES):
                    seen(e, "m_xT", L, i.val + 1)
                    if not i.first(UM):
                        seen(e, "m_up", L, 2 * (i.val - 3))
                    src = ps[:, 5, 0:2 * P].rearrange("p (c t) -> p c t", c=2)
                    e.copy(xgTh[i.par][0:HD, 0, :], src[0:HD, 0, :]).then_inc(sem("m_xc"), 1)
                    e.copy(xgTh[i.par][:, 1, :], src[0:HD + 1, 1, :]).then_inc(sem("m_xc"), 1)
                i = k + 1
                if i.live(TILES):
                    for b in range(2):
                        seen(e, "m_up", L, 2 * i.val + b + 1)
                        if b == 0 and not i.first(1):
                            seen(e, "m_hT", L, i.val)
                        e.activation(hact[:, b * (F // 2):(b + 1) * (F // 2)], ps[:, b, 0:F // 2], func
                                     ).then_inc(sem("m_act"), 1)
            steps(e, step, **EXP)

        def exp_vector(e, L):
            if L == 0:
                e.wait_ge(sem("vrow"), 1)
                a3 = avec[:, :].rearrange("s (t c) -> s t c", c=2)
                e.memset(a3[:, :, 1], -1.0).then_inc(sem("chain"), 1)
                e.scalar_tensor_tensor(out=a3[:, :, 0], in0=ps[0:2 * S, 6, 0:T], scalar=-2.0,
                                       in1=cst[0:2 * S, C_ALT:C_ALT + T], op0=ALU.add, op1=ALU.mult
                                       ).then_inc(sem("chain"), 1)
                e.wait_ge(sem("chain"), 2)
                e.tensor_copy(cur[0][:, :], avec[:, 0:2]).then_inc(sem("chain"), 1)
                e.tensor_copy(xy[:, 0:2], avec[:, 0:2]).then_inc(sem("chain0"), 1)
            e.wait_ge(sem(f"we_in{L}"), 48)

            def chain(k, u):
                t = 2 * k.val + u + 1
                done = 4 * (2 * k.val + u) + 3
                a, b = cur[u], cur[1 - u]
                e.wait_ge(sem("chain"), done)
                e.tensor_tensor_reduce(sqj[:, :], a[:, :], a[:, :], 1.0, 0.0, ALU.mult, ALU.add,
                                       nrm[:, 0:1]).then_inc(sem("chain"), 1)
                e.wait_ge(sem("chain"), done + 1)
                e.reciprocal(nrm[:, 1:2], nrm[:, 0:1]).then_inc(sem("chain"), 1)
                e.wait_ge(sem("chain"), done + 2)
                e.scalar_tensor_tensor(out=b[:, :], in0=a[:, :], scalar=nrm[:, 1:2], in1=avec[:, bass.ds(2 * t, 2)],
                                       op0=ALU.mult, op1=ALU.add).then_inc(sem("chain"), 1)
                e.wait_ge(sem("chain"), done + 3)
                e.tensor_copy(xy[:, bass.ds(2 * t, 2)], b[:, :]).then_inc(sem("chain"), 1)

            def low(i):
                if i.live(TILES):
                    seen(e, "m_xc", L, 2 * i.val + 2)
                    src = ps[:, 5, 0:2 * P].rearrange("p (c t) -> p c t", c=2)
                    e.tensor_tensor(xgTl[i.par][0:HD, 0, :], src[0:HD, 0, :], xgTh[i.par][0:HD, 0, :], ALU.subtract)
                    e.tensor_tensor(xgTl[i.par][:, 1, :], src[0:HD + 1, 1, :], xgTh[i.par][:, 1, :],
                                    ALU.subtract).then_inc(sem("m_xl"), 1)
            low(Idx(0, 0, UM))
            low(Idx(0, 1, UM))

            def step(k, with_chain):
                low(k + 2)
                i = k
                seen(e, "m_hT", L, i.val + 1)
                if not i.first(1):
                    seen(e, "m_dn", L, i.val)
                e.tensor_copy(hTs[:, 3:, :], ps[:, 3, 0:3 * P].rearrange("p (c t) -> p c t", c=3)).then_inc(sem("m_hd"), 1)
                if with_chain:
                    chain(k, 0)
                    chain(k, 1)
                ex = expert_of(e, i)
                seen(e, "m_dn", L, i.val + 1)
                e.tensor_tensor(yb[:, :], ps[:, 4, 0:D], b2[:, bass.ds(ex * D, D)], ALU.add).then_inc(sem("m_y"), 1)
                seen(e, "m_y", L, i.val + 1)
                if not i.first(UM):
                    seen(e, "m_sc", L, 16 * (i.val - 3))
                e.tensor_scalar(yw[i.par][:, :], yb[:, :], xg[i.par][:, bass.ds(ex + (D + 1), 1)], None,
                                ALU.mult).then_inc(sem("m_yw"), 1)
            if L == 0:
                assert CHAIN_TILES % UM == 0 and CHAIN_PER_TILE * CHAIN_TILES == T - 1
                steps(e, lambda k: step(k, True), first=0, last=CHAIN_TILES - 1, whole=(UM, CHAIN_TILES - 1), U=UM)
                for k in range(CHAIN_TILES, TILES):
                    step(Idx(0, k, UM), False)
            else:
                steps(e, lambda k: step(k, False), first=0, last=TILES - 1, whole=(4, TILES - 1 - 4), U=UM)

        ROUTE_COMB, ROUTE_ALL = {}, {}

        @block.vector
        def _(e):
            tok_vector(e)
            for L in range(2):
                att_vector(e, L)
                ROUTE_ALL[L] = route_vector(e, L)
                ROUTE_COMB[L] = ROUTE_ALL[L] - 6
                exp_vector(e, L)

        @block.scalar
        def _(e):
            tok_scalar(e)
            for L in range(2):
                att_scalar(e, L)
                split_scalar(e, L)
                route_scalar(e, L)
                exp_scalar(e, L)

        @block.tensor
        def _(e):
            tok_tensor(e)
            for L in range(2):
                att_tensor(e, L)
                route_tensor(e, L)
                exp_tensor(e, L)

        @block.gpsimd
        def _(e):
            tok_pool(e)
            for L in range(2):
                att_pool(e, L)
                split_pool(e, L)
                exp_pool(e, L)

        @block.sync
        def _(e):
            tok_sync(e)
            for L in range(2):
                att_sync(e, L)
                route_sync(e, L)


def _constants():
    import numpy as np
    c = np.zeros((P, C_END), np.float32)
    p = np.arange(P)
    c[:, C_EYE:C_EYE + P] = np.eye(P)
    c[:, C_TRI:C_TRI + P] = p[:, None] < p[None, :]
    c[:, C_ONE:C_ONE + P] = 1
    c[:, C_IOTA:C_IOTA + P] = p
    c[:T, C_REV:C_REV + T] = np.eye(T)[::-1]
    c[:, C_P1] = p + 1
    c[:, C_IOT:C_IOT + TILES] = np.arange(TILES)
    c[:, C_IOB:C_IOB + S] = np.arange(S)
    c[:, C_KEY:C_KEY + E] = E - np.arange(E)
    c[:, C_CEIL:C_CEIL + NCEIL] = P * np.arange(NCEIL)
    c[:, C_RST:C_RST + E * S] = np.tile(np.arange(S) > 0, E)
    c[:, C_ALT:C_ALT + T] = 1 - 2 * (np.arange(T) % 2)
    c[:, C_NHALF:C_NHALF + S] = -0.5
    c[S:2 * S, C_SEL:C_SEL + S] = np.eye(S)
    return c


def _rim(a, fill=0):
    import numpy as np
    q = PATCH
    lead = a.shape[:-3]
    parts = (a[..., 1:q + 1, 1:q + 1, :], a[..., 0, 1:q + 1, :], a[..., q + 1, 1:q + 1, :],
             a[..., 1:q + 1, 0, :], a[..., 1:q + 1, q + 1, :])
    return np.concatenate([x.reshape(*lead, -1) for x in parts], axis=-1)


def _layout(a):
    import numpy as np
    q = PATCH
    z = lambda *s: np.zeros(s, np.float32)
    out = {"consts": _constants()}
    x = z(S, 98, 98, CH)
    x[:, 1:-1, 1:-1] = a["x"]
    win = np.stack([np.stack([x[:, h * q:h * q + q + 2, w * q:w * q + q + 2] for w in range(6)], 1)
                    for h in range(6)], 1)
    out["pixels"] = _rim(win).reshape(S * NPATCH, NPIX)
    off = [(0, 0), (0, -1), (0, 1), (-1, 0), (1, 0)]

    def spread(v):
        v = v.reshape(q, q, SHIFTS, CH, -1)
        r = np.zeros((SHIFTS, v.shape[-1], q + 2, q + 2, CH), v.dtype)
        for s, (di, dj) in enumerate(off):
            r[s, :, 1 + di:1 + di + q, 1 + dj:1 + dj + q] = v[:, :, s].transpose(3, 0, 1, 2)
        return _rim(r).transpose(0, 2, 1)

    cols = lambda v: np.ascontiguousarray(v.reshape(SHIFTS, NK, KP, -1).transpose(0, 2, 1, 3))
    out["tok_w"] = cols(spread(a["L0_tok_W"]))
    gb = [cols(spread(a[k][:, None]))[..., 0].transpose(1, 0, 2) for k in ("L0_tok_gamma", "L0_tok_beta")]
    out["tok_gb"] = np.ascontiguousarray(np.stack(gb, 1))
    one = np.ones((q * q * SHIFTS * CH, 1), np.int64)
    m = spread(one)[..., 0]
    out["mult"] = np.tile((m > 0).sum(0).astype(np.float32)[None], (P, 1))
    out["L0_tok_b"] = a["L0_tok_b"]
    out["txt"] = a["txt"]
    halves = lambda w: np.ascontiguousarray(w.reshape(2, HD, -1).transpose(1, 0, 2))
    for L in range(2):
        w = a[f"L{L}_attn_w_qkv"].reshape(3, G, R, DH, D)
        pad = z(2, G, R, 32, D)
        pad[:, :, :, :DH] = w[:2]
        out[f"wqk{L}"] = halves(pad.reshape(2 * G * P, D).T).reshape(HD, 2, 2 * G, P)
        out[f"wv{L}"] = halves(w[2].reshape(D, D).T)
        for k in (f"wqk{L}", f"wv{L}"):
            out[k] = np.concatenate([out[k], z(P - HD, *out[k].shape[1:])])
        wp = a[f"L{L}_attn_w_proj"].T
        if L == 0:
            out["wpr0"] = halves(wp)
        else:
            pad = z(G, R, 32, D)
            pad[:, :, :DH] = wp.reshape(G, R, DH, D)
            out["wpr1"] = np.ascontiguousarray(pad.reshape(G, P, D).transpose(1, 0, 2))
        out[f"bpr{L}"] = np.tile(a[f"L{L}_attn_b_proj"][None], (T, 1))
        g = z(D + 2, E + 1)
        if L == 0:
            g[:D, :E] = a["L0_ffn_gate_w"]
            g[:D, E] = a["L0_ffn_v_w"]
            g[D, :E] = a["L0_ffn_gate_b"]
            g[D, E] = a["L0_ffn_v_b"]
        else:
            g[:D, :E] = a["L1_ffn_Wr"]
        wg = z(HD + 1, 2, E + 1)
        wg[:HD, 0], wg[:, 1] = g[:HD], g[HD:D + 1]
        out[f"wg{L}"] = wg
        u1, c1, u2, c2 = [a[f"L0_ffn_{k}" if L == 0 else f"L1_ffn_{k}"] for k in
                          (("w1", "b1", "w2", "b2") if L == 0 else ("W1", "b1", "W2", "b2"))]
        wu = z(HD + 1, 2, E, F)
        wu[:HD] = u1.reshape(E, 2, HD, F).transpose(2, 1, 0, 3)
        wu[HD, 1] = c1
        out[f"w1_{L}"] = wu.reshape(HD + 1, 2, E * F)
        out[f"w2_{L}"] = np.ascontiguousarray(u2.reshape(E * FC, P, D).transpose(1, 0, 2))
        out[f"b2_{L}"] = np.tile(c2.reshape(1, E * D), (P, 1))
    out["spec_w"] = np.concatenate([a["L0_ffn_out_w"], a["L0_ffn_out_b"][None]], 0)
    out["spec_s"] = np.tile(a["L0_ffn_bk_scale"][None], (3, 1))
    return {k: np.ascontiguousarray(v) for k, v in out.items()}


def kernel(**inputs):
    import numpy as np
    import concourse.bacc as bacc
    from concourse.bass_utils import run_bass_kernel_spmd

    laid = _layout({k: np.asarray(v) for k, v in inputs.items()})
    nc = bacc.Bacc("TRN2", target_bir_lowering=False, num_devices=1)
    arrays, aps = {}, {}
    for name, v in laid.items():
        arrays[f"in_{name}"] = v
        aps[name] = nc.dram_tensor(f"in_{name}", v.shape, mybir.dt.from_np(v.dtype), kind="ExternalInput").ap()
    out = nc.dram_tensor("out", (S, T, D), F32, kind="ExternalOutput").ap()
    fusion_kernel(nc, aps, out)
    r = run_bass_kernel_spmd(nc, [arrays], core_ids=[0])
    return r.results[0]["out"]
```

```python
from contextlib import ExitStack

import concourse.bass as bass
from concourse import mybir

F32 = mybir.dt.float32
F32R = mybir.dt.float32r
BF16 = mybir.dt.bfloat16
I32 = mybir.dt.int32
U32 = mybir.dt.uint32
ALU = mybir.AluOpType
ACT = mybir.ActivationFunctionType
AX = mybir.AxisListType

P = 128
S = 32
PATCH, CH, SHIFTS = 16, 3, 5
NPATCH = 36
NTXT = 77
T = NPATCH + NTXT
N = S * T
D = 192
HD = D // 2
HEADS, DH = 12, 16
G, R = 3, 4
E, F = 8, 768
FC = F // P
NF = PATCH * PATCH * SHIFTS * CH
NPIX = PATCH * PATCH * CH + 4 * PATCH * CH
KP = 120
NK = NPIX // KP
NTOK = S * NPATCH // P
TILES = 2 * N // P + E
ROW = 208
EPS_TOK, EPS = 1e-3, 1e-5
V_MAX, FEAT_MAX = 3.0, 10.0
UNUSED = 8192

C_EYE, C_TRI, C_ONE, C_IOTA, C_REV = 0, 128, 256, 384, 512
C_P1 = 640
C_IOT = C_P1 + 1
C_KEY = C_IOT + TILES
C_CEIL = C_KEY + E
NCEIL = N // P + 1
C_RST = C_CEIL + NCEIL
C_ALT = C_RST + E * S
C_NHALF = C_ALT + T
C_SEL = C_NHALF + S
C_LOW = C_SEL + S
C_HALF = C_LOW + 2
C_END = C_HALF + 1
FR = 9
FEAT_OPS = 18
CHAIN_PER_TILE = 2
CHAIN_TILES = (T - 1) // CHAIN_PER_TILE


class Idx:

    def __init__(self, m, c, U, B=None):
        self.m, self.c, self.U, self.B = m, c, U, B or U

    def __add__(self, o):
        return Idx(self.m, self.c + o, self.U, self.B)

    @property
    def val(self):
        return self.c if isinstance(self.m, int) and self.m == 0 else self.U * self.m + self.c

    @property
    def par(self):
        return self.c % self.B

    @property
    def turn(self):
        q = self.c // self.B
        return q if isinstance(self.m, int) and self.m == 0 else self.m * (self.U // self.B) + q

    def live(self, n):
        return not (isinstance(self.m, int) and self.m == 0) or 0 <= self.c < n

    def first(self, n):
        return isinstance(self.m, int) and self.m == 0 and self.c < n


def steps(eng, body, first, last, whole, U, B=None):
    lo = -(-whole[0] // U)
    hi = max(lo, (whole[1] + 1) // U)
    for k in range(first, lo * U):
        body(Idx(0, k, U, B))
    if hi > lo:
        with eng.Fori(lo, hi) as m:
            for u in range(U):
                body(Idx(m, u, U, B))
    for k in range(hi * U, last + 1):
        body(Idx(0, k, U, B))


def fusion_kernel(nc, ins, out):
    with ExitStack() as ctx:
        def sb(name, shape, dt=F32):
            return ctx.enter_context(nc.sbuf_tensor(name, shape, dt))

        def dram(name, shape, dt=F32):
            return nc.dram_tensor(name, shape, dt, kind="Internal").ap()

        sems = {}

        def sem(name):
            if name not in sems:
                sems[name] = ctx.enter_context(nc.semaphore(name))
            return sems[name]

        tok_d = dram("tok_d", (S * NPATCH, D))
        rows_d = [dram(f"rows_d{L}", (N, ROW)) for L in range(2)]
        acc_d = [dram("acc_d", (N, D)), out.rearrange("s t d -> (s t) d")]
        feat_d = dram("feat_d", (FR, N))

        ps = ctx.enter_context(nc.psum_tensor("ps", [P, 8, 512], F32))
        cst = sb("cst", [P, C_END])
        eye = cst[:, C_EYE:C_EYE + P]
        ones_bf = sb("ones_bf", [P, P], BF16)
        tri_bf = sb("tri_bf", [P, P], BF16)
        UT = 3
        with ExitStack() as early:
            def tb(name, shape, dt=F32):
                return early.enter_context(nc.sbuf_tensor(name, shape, dt))
            wsh = tb("wsh", [KP, SHIFTS, NK, D])
            gam = tb("gam", [KP, 2, SHIFTS, NK])
            weff = tb("weff", [KP, NK, D])
            mult = tb("mult", [P, NPIX])
            pix = [tb(f"pix{i}", [P, NPIX]) for i in range(UT)]
            cen = [tb(f"cen{i}", [P, NPIX]) for i in range(UT)]
            sq = tb("sq", [P, NPIX])
            zT = [tb(f"zT{i}", [KP, NK, P]) for i in range(UT)]
            tmu = [tb(f"tmu{i}", [P, 4]) for i in range(UT)]
            tout = [tb(f"tout{i}", [P, D]) for i in range(UT)]
            brow = tb("brow", [1, D])
            tokb = tb("tokb", [1, D])
            tbias = tb("tbias", [P, D])
        w1 = sb("w1", [HD + 1, 2, E * F])
        w2 = sb("w2", [P, E * FC, D])
        b2 = sb("b2", [P, E * D])
        wpr = sb("wpr", [HD, 2, D])
        bpr = sb("bpr", [T, D])
        wg = sb("wg", [HD + 1, 2, E + 1])
        lgt = sb("lgt", [T, S * (E + 1)])
        epst = sb("epst", [P, 2])

        def load(q, dst, src, s, n=16):
            q.dma_start(dst, src).then_inc(sem(s), n)

        UA = 4
        bst = [sb(f"bst{i}", [T, 6]) for i in range(2)]
        bs2 = [sb(f"bs2{i}", [T, 6]) for i in range(2)]
        mv1 = [sb(f"mv1{i}", [T, 4]) for i in range(2)]
        mv2 = [sb(f"mv2{i}", [T, 4]) for i in range(2)]
        xn = [sb(f"xn{i}", [T, D]) for i in range(2)]
        hb = [sb(f"hb{i}", [T, D]) for i in range(2)]
        h2 = [sb(f"h2{i}", [T, D]) for i in range(UA)]
        x2 = [sb(f"x2{i}", [T, ROW]) for i in range(UA)]
        x2T = [sb(f"x2T{i}", [HD + 1, 2, T]) for i in range(2)]
        psc = sb("psc", [T, D])
        wprb = sb("wprb", [P, G, D], BF16)
        wraw = sb("wraw", [P, G, D])
        avec = sb("avec", [2 * S, T * 2])
        xy = sb("xy", [2 * S, T * 2])
        cur = [sb(f"cur{i}", [2 * S, 2]) for i in range(2)]
        sqj = sb("sqj", [2 * S, 2])
        nrm = sb("nrm", [2 * S, 2])
        gidx = sb("gidx", [P, TILES], U32)
        sidx = sb("sidx", [P, TILES], U32)
        eti = sb("eti", [1, TILES], I32)

        def tb(name, shape, dt=F32):
            return phase.enter_context(nc.sbuf_tensor(name, shape, dt))

        def ab(name, shape, dt=F32):
            return mid.enter_context(nc.sbuf_tensor(name, shape, dt))

        with ExitStack() as phase:
            H = tb("H", [T, S * D])
            wqh = tb("wqh", [P, 2, 2 * G, P], F32R)
            wql = tb("wql", [P, 2, 2 * G, P], F32R)
            wvh = tb("wvh", [P, 2, D], F32R)
            wvl = tb("wvl", [P, 2, D], F32R)
            wqr = tb("wqr", [P, 2, 2 * G, P])
            wvr = tb("wvr", [P, 2, D])
            xTh = [tb(f"xTh{i}", [P, 2, 2, T], F32R) for i in range(2)]
            xTl = [tb(f"xTl{i}", [P, 2, 2, T], F32R) for i in range(2)]
            with ExitStack() as mid:
                qT = [ab(f"qT{i}", [P, G, 2, T]) for i in range(2)]
                kT = [ab(f"kT{i}", [P, G, 2, T]) for i in range(2)]
                vv = [ab(f"vv{i}", [T, HEADS, 2 * DH]) for i in range(2)]
                avT = ab("avT", [P, G * T])
                mx = ab("mx", [T, HEADS])
                pr = ab("pr", [T, R, G, T])
                pT = ab("pT", [T, R, G, T])
                rs = ab("rs", [T, HEADS])
                on = ab("on", [T, HEADS, DH])
                oT = ab("oT", [HD, 2, T])
            with ExitStack() as mid:
                feat = ab("feat", [S, 7, T])
                fT = ab("fT", [FR, N], F32R)
                spw = ab("spw", [FR, D])
                bks = ab("bks", [FR, D])
                spg = ab("spg", [FR, D])
                sph = ab("sph", [FR, D], F32R)
                spl = ab("spl", [FR, D], F32R)
                sps = ab("sps", [FR, D], F32R)
                waq = ab("waq", [HD, 2, 2 * G * P], F32R)
                wav = ab("wav", [HD, 2, D], F32R)
                onesr = ab("onesr", [P, P], F32R)
                fea = ab("fea", [S, FR, T], F32R)
                wap = ab("wap", [P, G, D])
            with ExitStack() as mid:
                qTb = [ab(f"qTb{i}", [P, G, 2, T], BF16) for i in range(2)]
                kTb = [ab(f"kTb{i}", [P, G, 2, T], BF16) for i in range(2)]
                vb = [ab(f"vb{i}", [T, HEADS, 2 * DH], BF16) for i in range(UA)]
                binq = [ab(f"binq{i}", [T, R, G, T], BF16) for i in range(2)]
                oTb = ab("oTb", [P, G, T], BF16)
                ypr = ab("ypr", [T, D])

        with ExitStack() as phase:
            w1h = tb("w1h", [HD + 1, 2, E * F], F32R)
            with ExitStack() as mid:
                key = ab("key", [T, S, E])
                lg2 = ab("lg2", [T, S, E])
                sel = [ab(f"sel{i}", [T, S, E]) for i in range(2)]
                top = [ab(f"top{i}", [T, S]) for i in range(2)]
                kmx = [ab(f"kmx{i}", [T, S]) for i in range(2)]
                wts = ab("wts", [T, 4, S])
                msk = ab("msk", [T, E, S], BF16)
                incl = ab("incl", [T, E, S])
                pos = ab("pos", [T, E, S])
                ceil = ab("ceil", [T, E, NCEIL])
                cnt = ab("cnt", [T, 4, E])
                slot = ab("slot", [T, 2, S])
                sli = ab("sli", [T, 3, 2 * S], I32)
                hilo = ab("hilo", [T, 2, 2 * S])
                CK = 8
                ohl = [ab(f"ohl{i}", [T, CK, P], BF16) for i in range(2)]
                ohh = [ab(f"ohh{i}", [T, CK, TILES], BF16) for i in range(2)]
                oht = [ab(f"oht{i}", [T, CK, 2, TILES], BF16) for i in range(2)]
                comb = ab("comb", [T, S, E])
                cmb2 = ab("cmb2", [T, S, E])
                et = ab("et", [1, TILES, E])
                etf = ab("etf", [1, TILES])
                tks = ab("tks", [P, 2, TILES])
                used = ab("used", [P, TILES])
                tid = ab("tid", [P, TILES])
                vcol = ab("vcol", [T, S])
            with ExitStack() as mid:
                UM = 4
                xg = [ab(f"xg{i}", [P, ROW]) for i in range(UM)]
                xgTh = [ab(f"xgTh{i}", [HD + 1, 2, P], F32R) for i in range(UM)]
                xgTl = [ab(f"xgTl{i}", [HD + 1, 2, P], F32R) for i in range(UM)]
                hact = ab("hact", [P, F])
                hTs = ab("hTs", [P, FC, P])
                yb = ab("yb", [P, D])
                yw = [ab(f"yw{i}", [P, D]) for i in range(UM)]
                gcur = [ab(f"gcur{i}", [P, 1], U32) for i in range(UM)]
                scur = [ab(f"scur{i}", [P, 1], U32) for i in range(UM)]

        left = dict.fromkeys("a_h2 a_x2 a_ln a_hb a_bs a_mv a_cs a_nv a_x2T a_xT a_av a_xl a_qm "
                             "a_v a_vc a_pj a_g a_gc a_xc a_oc".split(), S)
        left |= dict.fromkeys("a_mvr a_nvr a_x2c a_qc a_s a_sub".split(), 2 * S)
        left |= dict.fromkeys([f"st_{x}{p}" for x in "hx" for p in range(UA)], 16 * (S // UA))
        left |= dict(a_yp=0, r_gap=1, r_cnt=1, r_exp=1, r_cw=7)
        left |= dict.fromkeys("r_l r_i r_oh".split(), 2 * S // CK) | {"r_h": 2 * (2 * S // CK)}
        left |= dict.fromkeys("m_gi m_si m_yw m_xT m_hT m_hc m_hd m_y m_dn m_xl".split(), TILES)
        left |= dict.fromkeys("m_act m_xc m_up".split(), 2 * TILES) | {"m_sc": 16 * TILES}
        left |= {f"m_g{p}": 16 * len(range(p, TILES, UM)) for p in range(UM)}

        def seen(eng, name, L, count):
            eng.wait_ge(sem(name), count + left[name] if L else count)

        def at(tile, i, n, width=None):
            return tile[:, bass.ds(i.val * n, width or n)]

        nhalf = cst[:, C_NHALF:C_NHALF + 1]
        block = ctx.enter_context(nc.Block())

        TOK = dict(first=-2, last=NTOK - 1, whole=(UT, NTOK - 1 - 2), U=UT)

        def tok_sync(e):
            load(e, cst[:, :], ins["consts"], "consts")
            load(e, gam[:, :, :, :], ins["tok_gb"], "gam_in")
            load(e, tokb[:, :], ins["L0_tok_b"].unsqueeze(0), "gam_in")
            load(e, mult[:, :], ins["mult"], "mult_in")
            for i in range(UT):
                load(e, pix[i][:, :], ins["pixels"][i * P:(i + 1) * P, :], f"pix_in{i}")
            for s in range(SHIFTS):
                load(e, wsh[:, s, :, :], ins["tok_w"][s], f"wsh_in{s}")
            Hv = H[:, :].rearrange("t (s d) -> t s d", d=D)
            load(e, Hv[NPATCH:T], ins["txt"].rearrange("s t d -> t s d"), "h_in0")
            load(e, wqr[:, :, :, :], ins["wqk0"], "w_in0")
            load(e, wvr[:, :, :], ins["wv0"], "w_in0")
            load(e, wpr[:, :, :], ins["wpr0"], "w_in0")
            load(e, bpr[:, :], ins["bpr0"], "w_in0")
            load(e, wg[:, :, :], ins["wg0"], "w_in0")

            def step(k):
                i = k + 5
                if i.c >= UT and i.live(NTOK):
                    e.wait_ge(sem("tk_cen"), i.val - 2)
                    load(e, pix[i.par][:, :], ins["pixels"][bass.ds(i.val * P, P), :], f"pix_in{i.par}")
                i = k
                if i.live(NTOK):
                    e.wait_ge(sem("tk_out"), i.val + 1)
                    load(e, tok_d[bass.ds(i.val * P, P), :], tout[i.par][:, :], f"tok_st{i.par}")
            steps(e, step, first=-2, last=NTOK - 1, whole=(UT, NTOK - 1 - 5), U=UT)

        def tok_pool(e):
            e.memset(epst[:, 0:1], EPS_TOK).then_inc(sem("eps_set"), 1)
            e.memset(epst[:, 1:2], EPS).then_inc(sem("eps_set"), 1)
            e.wait_ge(sem("consts"), 16)
            e.wait_ge(sem("eps_set"), 2)

            def step(k):
                i = k + 2
                if i.live(NTOK):
                    mu = tmu[i.par]
                    e.wait_ge(sem("tk_var"), i.val + 1)
                    e.tensor_tensor(mu[:, 2:3], mu[:, 1:2], epst[:, 0:1], ALU.add).then_inc(sem("tk_rs"), 1)
                    e.wait_ge(sem("tk_rs"), 2 * i.val + 1)
                    e.tensor_tensor(mu[:, 3:4], mu[:, 2:3], nhalf, ALU.pow).then_inc(sem("tk_rs"), 1)
            steps(e, step, **TOK)

        def tok_vector(e):
            e.wait_ge(sem("consts"), 16)
            e.tensor_copy(ones_bf[:, :], cst[:, C_ONE:C_ONE + P]).then_inc(sem("masks"), 1)
            e.tensor_copy(tri_bf[:, :], cst[:, C_TRI:C_TRI + P]).then_inc(sem("masks"), 1)

            def weights():
                e.wait_ge(sem("gam_in"), 32)
                for s in range(SHIFTS):
                    e.wait_ge(sem(f"wsh_in{s}"), 16)
                    for k in range(NK):
                        if s == 0:
                            e.tensor_scalar(weff[:, k, :], wsh[:, s, k, :], gam[:, 0, s, k:k + 1], None,
                                            ALU.mult).then_inc(sem("weff"), 1)
                        else:
                            e.wait_ge(sem("weff"), (s - 1) * NK + k + 1)
                            e.scalar_tensor_tensor(out=weff[:, k, :], in0=wsh[:, s, k, :],
                                                   scalar=gam[:, 0, s, k:k + 1], in1=weff[:, k, :],
                                                   op0=ALU.mult, op1=ALU.add).then_inc(sem("weff"), 1)
                e.wait_ge(sem("beta_w"), 1)
                e.tensor_tensor(brow[:, :], ps[0:1, 7, 0:D], tokb[:, :], ALU.add).then_inc(sem("brow"), 1)
                e.wait_ge(sem("beta_b"), 1)
                e.tensor_copy(tbias[:, :], ps[:, 7, 0:D]).then_inc(sem("tbias"), 1)

            def centre(i):
                mu = tmu[i.par]
                e.wait_ge(sem(f"pix_in{i.par}"), 16 * (i.turn + 1))
                if not i.first(UT):
                    e.wait_ge(sem("tk_T"), i.val - 2)
                e.tensor_tensor_reduce(cen[i.par][:, :], pix[i.par][:, :], mult[:, :], 1.0 / NF, 0.0,
                                       ALU.mult, ALU.add, mu[:, 0:1]).then_inc(sem("tk_mu"), 1)
                e.wait_ge(sem("tk_mu"), i.val + 1)
                e.tensor_scalar(cen[i.par][:, :], pix[i.par][:, :], mu[:, 0:1], None,
                                ALU.subtract).then_inc(sem("tk_cen"), 1)

            def step(k):
                i = k + 2
                if i.live(NTOK):
                    if i.first(1):
                        e.wait_ge(sem("mult_in"), 16)
                    centre(i)
                i = k + 1
                if i.live(NTOK):
                    e.wait_ge(sem("tk_T"), i.val + 1)
                    if not i.first(2):
                        e.wait_ge(sem("tk_mm"), i.val - 1)
                    e.tensor_copy(zT[i.par][:, NK // 2:, :],
                                  ps[0:KP, 2 * i.par + 1, :].rearrange("p (k t) -> p k t", t=P)
                                  ).then_inc(sem("tk_zd"), 1)
                i = k + 2
                if i.live(NTOK):
                    e.wait_ge(sem("tk_sq"), i.val + 1)
                    e.tensor_tensor_reduce(sq[:, :], sq[:, :], mult[:, :], 1.0 / NF, 0.0,
                                           ALU.mult, ALU.add, tmu[i.par][:, 1:2]).then_inc(sem("tk_var"), 1)
                i = k
                if i.live(NTOK):
                    if i.first(1):
                        weights()
                        e.wait_ge(sem("tbias"), 1)
                    e.wait_ge(sem("tk_mm"), i.val + 1)
                    e.wait_ge(sem("tk_rs"), 2 * i.val + 2)
                    if not i.first(UT):
                        e.wait_ge(sem(f"tok_st{i.par}"), 16 * i.turn)
                    e.scalar_tensor_tensor(out=tout[i.par][:, :], in0=ps[:, 6, 0:D], scalar=tmu[i.par][:, 3:4],
                                           in1=tbias[:, :], op0=ALU.mult, op1=ALU.add).then_inc(sem("tk_out"), 1)
            steps(e, step, **TOK)

        def tok_scalar(e):
            def step(k):
                i = k + 2
                if i.live(NTOK):
                    e.wait_ge(sem("tk_cen"), i.val + 1)
                    if not i.first(1):
                        e.wait_ge(sem("tk_var"), i.val)
                    e.activation(sq[:, :], cen[i.par][:, :], ACT.Square).then_inc(sem("tk_sq"), 1)
                i = k + 1
                if i.live(NTOK):
                    e.wait_ge(sem("tk_T"), i.val + 1)
                    if not i.first(2):
                        e.wait_ge(sem("tk_mm"), i.val - 1)
                    e.copy(zT[i.par][:, 0:NK // 2, :],
                           ps[0:KP, 2 * i.par, :].rearrange("p (k t) -> p k t", t=P)).then_inc(sem("tk_za"), 1)
            steps(e, step, **TOK)

        def tok_tensor(e):
            e.wait_ge(sem("consts"), 16)

            def beta():
                e.wait_ge(sem("gam_in"), 32)
                for s in range(SHIFTS):
                    e.wait_ge(sem(f"wsh_in{s}"), 16)
                    for k in range(NK):
                        mm = e.matmul(ps[0:1, 7, 0:D], gam[:, 1, s, k:k + 1], wsh[:, s, k, :],
                                      start=(s == 0 and k == 0), stop=(s == SHIFTS - 1 and k == NK - 1))
                mm.then_inc(sem("beta_w"), 1)
                e.wait_ge(sem("brow"), 1)
                e.matmul(ps[:, 7, 0:D], cst[0:1, C_ONE:C_ONE + P], brow[:, :],
                         start=True, stop=True).then_inc(sem("beta_b"), 1)

            def step(k):
                i = k + 1
                if i.live(NTOK):
                    e.wait_ge(sem("tk_cen"), i.val + 1)
                    if not i.first(2):
                        e.wait_ge(sem("tk_za"), i.val - 1)
                        e.wait_ge(sem("tk_zd"), i.val - 1)
                    for c in range(NK):
                        mm = e.transpose(ps[0:KP, 2 * i.par + c // 4, (c % 4) * P:(c % 4 + 1) * P],
                                         cen[i.par][:, c * KP:(c + 1) * KP], eye)
                    mm.then_inc(sem("tk_T"), 1)
                i = k
                if i.live(NTOK):
                    if i.first(1):
                        beta()
                        e.wait_ge(sem("weff"), SHIFTS * NK)
                    else:
                        e.wait_ge(sem("tk_out"), i.val)
                    e.wait_ge(sem("tk_za"), i.val + 1)
                    e.wait_ge(sem("tk_zd"), i.val + 1)
                    for c in range(NK):
                        mm = e.matmul(ps[:, 6, 0:D], zT[i.par][:, c, :], weff[:, c, :],
                                      start=(c == 0), stop=(c == NK - 1))
                    mm.then_inc(sem("tk_mm"), 1)
            steps(e, step, **TOK)

        AHEAD = (dict(stat=6, x=5, part=3, v=2), dict(stat=7, x=6, part=4, v=4))
        ATT = [dict(first=-AHEAD[L]["stat"], last=S, whole=(4, S - 1 - AHEAD[L]["stat"]), U=UA) for L in range(2)]

        HALVES = (slice(0, R // 2), slice(R // 2, R))

        def att_sync(e, L):
            Hv = H[:, :].rearrange("t (s d) -> t s d", d=D)
            if L == 0:
                for p in range(UT):
                    e.wait_ge(sem(f"tok_st{p}"), 16 * (NTOK // UT))
                load(e, Hv[0:NPATCH], tok_d.rearrange("(s t) d -> t s d", t=NPATCH), "h_in0")
                e.wait_ge(sem("tk_mm"), NTOK)
            else:
                seen(e, "m_dn", 0, TILES)
                load(e, wqr[:, :, :, :], ins["wqk1"], "w_in1")
                load(e, wvr[:, :, :], ins["wv1"], "w_in1")
                load(e, wraw[:, :, :], ins["wpr1"], "w_in1")
                load(e, bpr[:, :], ins["bpr1"], "w_in1")
                load(e, wg[:, :, :], ins["wg1"], "w_in1")
                load(e, spw[:, :], ins["spec_w"], "sp_in")
                load(e, bks[:, :], ins["spec_s"], "sp_in")
                e.wait_ge(sem("feats"), FEAT_OPS)
                load(e, feat_d.rearrange("c (s t) -> s c t", t=T), fea[:, :, :].bitcast(F32), "feat_st")
                e.wait_ge(sem("feat_st"), 16)
                e.wait_ge(sem("m_sc"), 16 * TILES)
                load(e, fT[:, :].bitcast(F32), feat_d, "feat_in")
            load(e, w1[:, :, :], ins[f"w1_{L}"], f"we_in{L}")
            load(e, w2[:, :, :], ins[f"w2_{L}"], f"we_in{L}")
            load(e, b2[:, :], ins[f"b2_{L}"], f"we_in{L}")

            def step(k):
                i = k
                if i.live(S):
                    seen(e, "a_h2", L, i.val + 1)
                    load(e, acc_d[L][bass.ds(i.val * T, T), :], h2[i.par][:, :], f"st_h{i.par}")
                i = k + -1
                if i.live(S):
                    seen(e, "a_x2", L, i.val + 1)
                    load(e, rows_d[L][bass.ds(i.val * T, T), :], x2[i.par][:, :], f"st_x{i.par}")
            steps(e, step, **ATT[L])

        def att_pool(e, L):
            st, xa, pa, va = (AHEAD[L][n_] for n_ in ("stat", "x", "part", "v"))
            if L == 0:
                for p in range(UA):
                    e.memset(x2[p][:, D:ROW], 0.0).then_inc(sem("x2_set"), 1)
                for p in range(2):
                    e.memset(vv[p][:, :, :], 1.0).then_inc(sem("v_set"), 1)
                e.wait_ge(sem("x2_set"), UA)
                for p in range(UA):
                    e.memset(x2[p][:, D:D + 1], 1.0).then_inc(sem("x2_set"), 1)
            else:
                e.wait_ge(sem("sp_mm"), S // 2)
                for p in range(UA):
                    e.memset(vb[p][:, :, :], 0.0).then_inc(sem("vb_set"), 1)
            e.wait_ge(sem(f"w_in{L}"), 80)

            def rstd(m, mv, i):
                seen(e, m, L, i.val + 1)
                e.tensor_tensor(mv[0:T, 2:3], mv[0:T, 1:2], epst[0:T, 1:2], ALU.add).then_inc(sem(m + "r"), 1)
                seen(e, m + "r", L, 2 * i.val + 1)
                e.tensor_tensor(mv[0:T, 3:4], mv[0:T, 2:3], nhalf[0:T], ALU.pow).then_inc(sem(m + "r"), 1)

            def summand(k):
                i = k + 1
                if i.live(S):
                    seen(e, "a_ln", L, i.val + 1)
                    if not i.first(2):
                        seen(e, "a_h2", L, i.val - 1)
                    e.tensor_tensor(hb[i.par % 2][:, :], at(H, i, D), bpr[:, :], ALU.add).then_inc(sem("a_hb"), 1)

            def step(k):
                i = k + st
                if i.live(S):
                    rstd("a_mv", mv1[i.par % 2], i)
                if L == 0:
                    summand(k)
                i = k
                if i.live(S):
                    mv = mv2[i.par % 2]
                    rstd("a_nv", mv, i)
                    if L == 1:
                        seen(e, "a_nvr", L, 2 * i.val + 2)
                        if not i.first(UA):
                            seen(e, f"st_x{i.par}", L, 16 * i.turn)
                            seen(e, "a_x2T", L, i.val - 3)
                if L == 1:
                    summand(k)
                    if i.live(S):
                        e.tensor_scalar(x2[i.par][:, 0:D], h2[i.par][:, :], mv[:, 0:1], mv[:, 3:4],
                                        ALU.subtract, ALU.mult).then_inc(sem("a_x2"), 1)
            steps(e, step, **ATT[L])

        def part_view(b):
            return (ps[:, 4, 0:4 * T] if b == 4 else ps[:, 5, 0:2 * T]).rearrange("p (g i t) -> p g i t", i=2, t=T)

        def qk_tile(L, j):
            if L == 0:
                return (qT, kT)[j.c % 2][j.c // 2 % 2]
            return (qTb, kTb)[j.c % 2][j.c // 2 % 2]

        def att_vector(e, L):
            st, xa, pa, va = (AHEAD[L][n_] for n_ in ("stat", "x", "part", "v"))
            if L == 0:
                e.wait_ge(sem("x2_set"), 2 * UA)
                e.wait_ge(sem("v_set"), 2)
                e.wait_ge(sem("wh"), 2)
                e.tensor_tensor(wql[:, :, :, :], wqr[:, :, :, :], wqh[:, :, :, :], ALU.subtract).then_inc(sem("wl"), 1)
                e.tensor_tensor(wvl[:, :, :], wvr[:, :, :], wvh[:, :, :], ALU.subtract).then_inc(sem("wl"), 1)
            else:
                prepare_vector(e)
            for p in range(2):
                e.memset(xTh[p][HD:P, :, :, :].bitcast(F32), 0.0).then_inc(sem("xz"), 1)
                e.memset(xTl[p][HD:P, :, :, :].bitcast(F32), 0.0).then_inc(sem("xz"), 1)
            e.wait_ge(sem(f"h_in{L}"), 32 if L == 0 else 16)

            def low(k):
                i = k + xa
                if i.live(S):
                    seen(e, "a_xc", L, i.val + 1)
                    pb = i.c // 2 % 2
                    e.tensor_tensor(xTl[pb][0:HD, :, i.c % 2, :], ps[0:HD, 4, 0:2 * T].rearrange("p (c t) -> p c t", c=2),
                                    xTh[pb][0:HD, :, i.c % 2, :], ALU.subtract).then_inc(sem("a_xl"), 1)

            def residual(k):
                i = k
                if i.live(S):
                    seen(e, "a_pj", L, i.val + 1)
                    seen(e, "a_hb", L, i.val + 1)
                    if not i.first(UA):
                        seen(e, f"st_h{i.par}", L, 16 * i.turn)
                    y = ps[0:T, 6, 0:D]
                    if L == 1:
                        e.tensor_tensor(ypr[:, :], y, psc[:, :], ALU.mult).then_inc(sem("a_yp"), 1)
                        seen(e, "a_yp", L, i.val + 1)
                        y = ypr[:, :]
                    e.tensor_tensor(h2[i.par][:, :], y, hb[i.par % 2][:, :], ALU.add).then_inc(sem("a_h2"), 1)
                    seen(e, "a_h2", L, i.val + 1)
                    e.bn_stats(bs2[i.par % 2][:, :], h2[i.par][:, :]).then_inc(sem("a_cs"), 1)
                    seen(e, "a_cs", L, i.val + 1)

            def step(k):
                i = k + xa
                if i.live(S):
                    mv = mv1[i.par % 2]
                    seen(e, "a_mvr", L, 2 * i.val + 2)
                    if not i.first(2):
                        seen(e, "a_xT", L, i.val - 1)
                    e.tensor_scalar(xn[i.par % 2][:, :], at(H, i, D), mv[:, 0:1], mv[:, 3:4],
                                    ALU.subtract, ALU.mult).then_inc(sem("a_ln"), 1)
                i = k + st
                if i.live(S):
                    e.bn_stats(bst[i.par % 2][:, :], at(H, i, D)).then_inc(sem("a_bs"), 1)
                i = k + 1
                if i.live(S) and L == 0:
                    for h, rr in enumerate(HALVES):
                        sc = ps[0:T, rr, 0:G * T].rearrange("n r (g m) -> n r g m", g=G)
                        mx3 = mx[:, :].rearrange("n (r g) -> n r g", r=R)[:, rr, :]
                        seen(e, "a_s", L, 2 * i.val + h + 1)
                        e.tensor_reduce(mx3, sc, AX.X, ALU.max).then_inc(sem("a_mx"), 1)
                        seen(e, "a_mx", L, 2 * i.val + h + 1)
                        e.tensor_tensor(pr[:, rr, :, :], sc, mx3.unsqueeze(3).broadcast_to([T, 2, G, T]),
                                        ALU.subtract).then_inc(sem("a_sub"), 1)
                for h, rr in enumerate(HALVES) if L == 1 else ():
                    if h == 1:
                        low(k)
                    if i.live(S):
                        seen(e, "a_s", L, 2 * i.val + h + 1)
                        sc = ps[0:T, rr, 0:G * T].rearrange("n r (g m) -> n r g m", g=G)
                        e.tensor_scalar(binq[i.par % 2][:, rr, :, :], sc, 0.0, None, ALU.is_gt).then_inc(sem("a_sub"), 1)
                i = k + -1
                if i.live(S) and L == 0:
                    mv = mv2[i.par % 2]
                    seen(e, "a_nvr", L, 2 * i.val + 2)
                    if not i.first(UA):
                        seen(e, f"st_x{i.par}", L, 16 * i.turn)
                        seen(e, "a_x2T", L, i.val - 3)
                    e.tensor_scalar(x2[i.par][:, 0:D], h2[i.par][:, :], mv[:, 0:1], mv[:, 3:4],
                                    ALU.subtract, ALU.mult).then_inc(sem("a_x2"), 1)
                if (k + st).live(S):
                    seen(e, "a_bs", L, (k + st).val + 1)
                i = k + va
                if i.live(S):
                    seen(e, "a_v", L, i.val + 1)
                    if not i.first(va):
                        seen(e, "a_av", L, i.val + 1 - va)
                    src = ps[0:T, 7, 0:D].rearrange("n (h d) -> n h d", h=HEADS)
                    if L == 0:
                        e.tensor_copy(vv[i.par % 2][:, :, 0:DH], src).then_inc(sem("a_vc"), 1)
                    else:
                        e.tensor_scalar(vb[i.par][:, :, 0:DH], src, 0.0, 0.5,
                                        ALU.is_ge, ALU.subtract).then_inc(sem("a_vc"), 1)
                i = k + st
                if i.live(S):
                    e.bn_aggr(mv1[i.par % 2][:, 0:2], bst[i.par % 2][:, :]).then_inc(sem("a_mv"), 1)
                if L == 1:
                    residual(k)
                j = k + pa
                if j.live(S) and L == 1:
                    seen(e, "a_qm", L, j.val + 1)
                    if not j.first(UA):
                        seen(e, "a_s", L, 2 * (j.val - 2))
                    for b, gs in ((4, slice(0, 2)), (5, slice(2, 3))):
                        e.tensor_scalar(qk_tile(L, j)[:, gs, :, :], part_view(b), 0.0, cst[:, C_HALF:C_HALF + 1],
                                        ALU.is_ge, ALU.subtract).then_inc(sem("a_qc"), 1)
                if L == 1 and k.live(S):
                    e.bn_aggr(mv2[k.par % 2][:, 0:2], bs2[k.par % 2][:, :]).then_inc(sem("a_nv"), 1)
                i = k
                if i.live(S) and L == 0:
                    av = ps[0:T, 6, 0:G * P].rearrange("n (h d) -> n h d", h=HEADS)
                    seen(e, "a_aT", L, i.val + 1)
                    e.reciprocal(rs[:, :], av[:, :, DH]).then_inc(sem("a_rc"), 1)
                    seen(e, "a_rc", L, i.val + 1)
                    if not i.first(1):
                        seen(e, "a_oT", L, i.val)
                    e.tensor_tensor(on[:, :, :], av[:, :, 0:DH], rs[:, :].unsqueeze(2).broadcast_to([T, HEADS, DH]),
                                    ALU.mult).then_inc(sem("a_on"), 1)
                i = k + 1
                if i.live(S) and L == 0:
                    seen(e, "a_pt", L, 2 * i.val + 2)
                    e.tensor_copy(pT[:, 2:4, :, :], ps[0:T, 2:4, 0:G * T].rearrange("m r (g n) -> m r g n", g=G)
                                  ).then_inc(sem("a_pd"), 1)
                if L == 0:
                    low(k)
                if L == 0:
                    residual(k)
                i = k + -1
                if i.live(S):
                    seen(e, "a_g", L, i.val + 1)
                    e.tensor_copy(at(lgt, i, E + 1), ps[0:T, 7, 0:E + 1]).then_inc(sem("a_gc"), 1)
                if L == 0 and k.live(S):
                    e.bn_aggr(mv2[k.par % 2][:, 0:2], bs2[k.par % 2][:, :]).then_inc(sem("a_nv"), 1)
            steps(e, step, **ATT[L])

        def att_scalar(e, L):
            st, xa, pa, va = (AHEAD[L][n_] for n_ in ("stat", "x", "part", "v"))
            if L == 0:
                e.wait_ge(sem("w_in0"), 80)
                e.copy(wqh[:, :, :, :], wqr[:, :, :, :]).then_inc(sem("wh"), 1)
                e.copy(wvh[:, :, :], wvr[:, :, :]).then_inc(sem("wh"), 1)
            else:
                prepare_scalar(e)

            def high(k):
                i = k + xa
                if i.live(S):
                    seen(e, "a_xT", L, i.val + 1)
                    if not i.first(UA):
                        seen(e, "a_v", L, i.val - 2)
                    e.copy(xTh[i.c // 2 % 2][0:HD, :, i.c % 2, :], ps[0:HD, 4, 0:2 * T].rearrange("p (c t) -> p c t", c=2)
                           ).then_inc(sem("a_xc"), 1)

            def step(k):
                def exp(h):
                    i = k + 1
                    if i.live(S) and L == 0:
                        seen(e, "a_sub", L, 2 * i.val + h + 1)
                        e.activation(pr[:, HALVES[h], :, :], pr[:, HALVES[h], :, :], ACT.Exp).then_inc(sem("a_e"), 1)
                exp(0)
                i = k
                if i.live(S):
                    seen(e, "a_av", L, i.val + 1)
                    if L == 0:
                        if not i.first(1):
                            seen(e, "a_aT", L, i.val)
                        e.copy(avT[:, :], ps[:, 6, 0:G * T]).then_inc(sem("a_ac"), 1)
                    else:
                        if not i.first(1):
                            seen(e, "a_pj", L, i.val)
                        e.copy(oTb[:, :, :], ps[:, 6, 0:G * T].rearrange("p (g t) -> p g t", g=G)
                               ).then_inc(sem("a_oc"), 1)
                exp(1)
                if L == 1:
                    high(k)
                i = k + 1
                if i.live(S) and L == 0:
                    seen(e, "a_pt", L, 2 * i.val + 1)
                    e.copy(pT[:, 0:2, :, :], ps[0:T, 0:2, 0:G * T].rearrange("m r (g n) -> m r g n", g=G)
                           ).then_inc(sem("a_pa"), 1)
                j = k + pa
                if j.live(S) and L == 0:
                    seen(e, "a_qm", L, j.val + 1)
                    if not j.first(UA):
                        seen(e, "a_s", L, 2 * (j.val - 2))
                    scale = 1.0 if j.c % 2 else DH ** -0.5
                    for b, gs in ((4, slice(0, 2)), (5, slice(2, 3))):
                        e.mul(qk_tile(L, j)[:, gs, :, :], part_view(b), scale).then_inc(sem("a_qc"), 1)
                i = k
                if i.live(S) and L == 0:
                    seen(e, "a_oT", L, i.val + 1)
                    if not i.first(1):
                        seen(e, "a_pj", L, i.val)
                    e.copy(oT[:, :, :], ps[0:HD, 6, 0:2 * T].rearrange("p (c t) -> p c t", c=2)).then_inc(sem("a_oc"), 1)
                i = k + -1
                if i.live(S):
                    seen(e, "a_x2T", L, i.val + 1)
                    if not i.first(2):
                        seen(e, "a_g", L, i.val - 1)
                    src = ps[:, 7, 0:2 * T].rearrange("p (c t) -> p c t", c=2)
                    e.copy(x2T[i.par % 2][0:HD, 0, :], src[0:HD, 0, :]).then_inc(sem("a_x2c"), 1)
                    e.copy(x2T[i.par % 2][:, 1, :], src[0:HD + 1, 1, :]).then_inc(sem("a_x2c"), 1)
                if L == 0:
                    high(k)
            steps(e, step, **ATT[L])

        def att_tensor(e, L):
            st, xa, pa, va = (AHEAD[L][n_] for n_ in ("stat", "x", "part", "v"))
            if L == 0:
                e.wait_ge(sem("wl"), 2)
            else:
                prepare_tensor(e)
                e.wait_ge(sem("signs"), 5)
            e.wait_ge(sem(f"w_in{L}"), 80)
            e.wait_ge(sem("xz"), 4 * (L + 1))
            passes = ((0, 0), (0, 1), (1, 0)) if L == 0 else ((0, 0), (0, 1))
            wq_, wv_, x_ = (wqh, wql), (wvh, wvl), (xTh, xTl)

            def turn(k, h):
                i = k + 1
                if i.live(S) and L == 0:
                    seen(e, "a_e", L, 2 * i.val + h + 1)
                    for r in range(HALVES[h].start, HALVES[h].stop):
                        for g in range(G):
                            mm = e.transpose(ps[0:T, r, g * T:(g + 1) * T], pr[:, r, g, :], eye[0:T, 0:T])
                    mm.then_inc(sem("a_pt"), 1)

            def turn_x(k):
                i = k + xa
                if i.live(S):
                    seen(e, "a_ln", L, i.val + 1)
                    last = k + (pa - L)
                    if last.live(S):
                        seen(e, "a_qc", L, 2 * last.val + 2)
                    elif not i.first(1):
                        seen(e, "a_xl", L, i.val)
                    e.transpose(ps[0:HD, 4, 0:T], xn[i.par % 2][:, 0:HD], eye[0:T, 0:T])
                    e.transpose(ps[0:HD, 4, T:2 * T], xn[i.par % 2][:, HD:D], eye[0:T, 0:T]).then_inc(sem("a_xT"), 1)

            def turn_x2(k):
                i = k + -1
                if i.live(S):
                    seen(e, "a_x2", L, i.val + 1)
                    if (k + va).live(S):
                        seen(e, "a_vc", L, (k + va).val + 1)
                    elif (k + -2).live(S):
                        seen(e, "a_gc", L, k.val - 1)
                    e.transpose(ps[0:HD, 7, 0:T], x2[i.par][:, 0:HD], eye[0:T, 0:T])
                    e.transpose(ps[0:HD + 1, 7, T:2 * T], x2[i.par][:, HD:D + 1],
                                eye[0:T, 0:T]).then_inc(sem("a_x2T"), 1)

            def part(k, g):
                j = k + pa
                if j.live(S):
                    if g == 0:
                        p = j.c // 2 * 2 - j.c
                        seen(e, "a_xl", L, j.val + p + 2)
                        if (j + 1 + L).live(S):
                            seen(e, "a_xl", L, (j + 1 + L).val + 1)
                        else:
                            seen(e, "a_qc", L, 2 * j.val)
                    n_ = 0
                    for c in range(2):
                        for a, b in passes:
                            mm = e.matmul(ps[:, 4 + g // 2, g % 2 * 2 * T:(g % 2 + 1) * 2 * T],
                                          wq_[a][:, c, G * (j.c % 2) + g, :],
                                          x_[b][j.c // 2 % 2][:, c, :, :].rearrange("p i t -> p (i t)"),
                                          start=(n_ == 0), stop=(n_ == 2 * len(passes) - 1))
                            n_ += 1
                    if g == 2:
                        mm.then_inc(sem("a_qm"), 1)

            def scores(k, h):
                i = k + 1
                if i.live(S):
                    if h == 0:
                        seen(e, "a_qc", L, 2 * (i.val + 2 - i.c % 2))
                    pb, u = i.c // 2 % 2, i.c % 2
                    q_, k_ = (qT[pb], kT[pb]) if L == 0 else (kTb[pb], qTb[pb])
                    if not i.first(1):
                        if L == 0:
                            seen(e, ("a_pa", "a_pd")[h], L, i.val)
                        else:
                            seen(e, "a_sub", L, 2 * i.val + h - 1)
                    for g in range(G):
                        for r in range(HALVES[h].start, HALVES[h].stop):
                            mm = e.matmul(ps[0:T, r, g * T:(g + 1) * T], q_[32 * r:32 * r + 32, g, u, :],
                                          k_[32 * r:32 * r + 32, g, u, :], start=True, stop=True)
                    mm.then_inc(sem("a_s"), 1)

            def project(k):
                i = k
                if i.live(S):
                    seen(e, "a_oc", L, i.val + 1)
                    if L == 0:
                        for c in range(2):
                            mm = e.matmul(ps[0:T, 6, 0:D], oT[:, c, :], wpr[:, c, :], start=(c == 0), stop=(c == 1))
                    else:
                        for g in range(G):
                            mm = e.matmul(ps[0:T, 6, 0:D], oTb[:, g, :], wprb[:, g, :],
                                          start=(g == 0), stop=(g == G - 1))
                    mm.then_inc(sem("a_pj"), 1)

            def step(k):
                for h in range(2):
                    scores(k, h)
                    if L == 0:
                        part(k, h)
                i = k
                if i.live(S):
                    seen(e, "a_vc", L, i.val + 1)
                    if not i.first(1):
                        seen(e, "a_h2" if L == 0 else "a_yp", L, i.val)
                    if L == 0:
                        seen(e, "a_pa", L, i.val + 1)
                        seen(e, "a_pd", L, i.val + 1)
                    else:
                        seen(e, "a_sub", L, 2 * i.val + 2)
                    for g in range(G):
                        for r in range(R):
                            v_ = vv[i.par % 2] if L == 0 else vb[i.par]
                            w_ = pT[:, r, g, :] if L == 0 else binq[i.par % 2][:, r, g, :]
                            mm = e.matmul(ps[32 * r:32 * r + 32, 6, g * T:(g + 1) * T], v_[:, R * g + r, :], w_,
                                          start=True, stop=True)
                    mm.then_inc(sem("a_av"), 1)
                if L == 1:
                    turn_x(k)
                i = k + va
                if i.live(S):
                    seen(e, "a_xl", L, i.val + 1)
                    if (k + -2).live(S):
                        seen(e, "a_gc", L, k.val - 1)
                    elif not i.first(1):
                        seen(e, "a_vc", L, i.val)
                    n_ = 2 * len(passes)
                    for c in range(2):
                        for a, b in passes:
                            n_ -= 1
                            mm = e.matmul(ps[0:T, 7, 0:D], x_[b][i.c // 2 % 2][:, c, i.c % 2, :], wv_[a][:, c, :],
                                          start=(n_ == 2 * len(passes) - 1), stop=(n_ == 0))
                    mm.then_inc(sem("a_v"), 1)
                turn(k, 0)
                if L == 1:
                    project(k)
                i = k
                if i.live(S) and L == 0:
                    seen(e, "a_ac", L, i.val + 1)
                    for g in range(G):
                        mm = e.transpose(ps[0:T, 6, g * P:(g + 1) * P], avT[:, g * T:(g + 1) * T], eye)
                    mm.then_inc(sem("a_aT"), 1)
                if L == 1:
                    part(k, 0)
                    part(k, 1)
                    turn_x2(k)
                part(k, 2)
                i = k
                if i.live(S) and L == 0:
                    seen(e, "a_on", L, i.val + 1)
                    o = on[:, :, :].rearrange("n h d -> n (h d)")
                    e.transpose(ps[0:HD, 6, 0:T], o[:, 0:HD], eye[0:T, 0:T])
                    e.transpose(ps[0:HD, 6, T:2 * T], o[:, HD:D], eye[0:T, 0:T]).then_inc(sem("a_oT"), 1)
                turn(k, 1)
                if L == 0:
                    turn_x2(k)
                if L == 0:
                    turn_x(k)
                if L == 0:
                    project(k)
                i = k + -1
                if i.live(S):
                    seen(e, "a_x2c", L, 2 * i.val + 2)
                    for c in range(2):
                        kk = HD + c
                        mm = e.matmul(ps[0:T, 7, 0:E + 1], x2T[i.par % 2][0:kk, c, :], wg[0:kk, c, :],
                                      start=(c == 0), stop=(c == 1))
                    mm.then_inc(sem("a_g"), 1)
            steps(e, step, **ATT[L])

        def prepare_scalar(e):
            e.wait_ge(sem("m_sc"), 16 * TILES)
            load(e, H[:, :].rearrange("t (s d) -> t s d", d=D), acc_d[0].rearrange("(s t) d -> t s d", t=T), "h_in1")
            e.wait_ge(sem("w_in1"), 80)
            e.copy(onesr[:, :], cst[:, C_ONE:C_ONE + P]).then_inc(sem("wabs"), 1)
            e.activation(waq[:, :, :], wqr[0:HD, :, :, :].rearrange("p c j o -> p c (j o)"), ACT.Abs).then_inc(sem("wabs"), 1)
            e.activation(wav[:, :, :], wvr[0:HD, :, :], ACT.Abs).then_inc(sem("wabs"), 1)
            e.activation(wap[:, :, :], wraw[:, :, :], ACT.Abs).then_inc(sem("wabs"), 1)

        def prepare_tensor(e):
            e.wait_ge(sem("chain"), 4 * (T - 1) + 3)
            e.matmul(ps[0:S, 6, 0:2 * T], cst[0:2 * S, C_SEL:C_SEL + S], xy[:, :], start=True,
                     stop=True).then_inc(sem("chain_b"), 1)
            half_w = G * P
            e.wait_ge(sem("wabs"), 4)
            for b in range(2):
                for c in range(2):
                    e.matmul(ps[:, b, 0:half_w], onesr[0:HD, :],
                             waq[:, c, b * half_w:(b + 1) * half_w], start=(c == 0), stop=(c == 1))
            for c in range(2):
                e.matmul(ps[:, 2, 0:D], onesr[0:HD, :], wav[:, c, :], start=(c == 0), stop=(c == 1))
            for g in range(G):
                mm = e.matmul(ps[0:T, 3, 0:D], cst[:, C_ONE:C_ONE + T], wap[:, g, :], start=(g == 0), stop=(g == G - 1))
            mm.then_inc(sem("abs_sum"), 1)
            e.wait_ge(sem("feat_in"), 16)
            e.wait_ge(sem("spg"), 5)
            for i in range(S):
                if i % 2 == 0 and i >= 8:
                    e.wait_ge(sem("sp_add"), i // 2 - 3)
                mm = e.matmul(ps[0:T, 4 + i // 2 % 4, (i % 2) * D:(i % 2 + 1) * D], fT[:, i * T:(i + 1) * T],
                              sps[:, :], start=True, stop=True)
                if i % 2:
                    mm.then_inc(sem("sp_mm"), 1)

        def prepare_vector(e):
            seq = [0]

            def chained(ins_):
                seq[0] += 1
                ins_.then_inc(sem("feats"), 1)
                e.wait_ge(sem("feats"), seq[0])

            fw = xy[0:S, :].rearrange("s (t c) -> s t c", c=2)
            av = avec[0:S, :].rearrange("s (t c) -> s t c", c=2)
            bw = ps[0:S, 6, 0:2 * T].rearrange("s (t c) -> s t c", c=2)
            alt = cst[0:S, C_ALT:C_ALT + T]
            e.wait_ge(sem("chain_b"), 1)
            f = [feat[:, j, :] for j in range(7)]
            chained(e.tensor_tensor(f[0], fw[:, :, 0], bw[:, ::-1, 0], ALU.add))
            chained(e.tensor_tensor(f[0], f[0], av[:, :, 0], ALU.subtract))
            chained(e.tensor_tensor(f[0], f[0], alt, ALU.mult))
            chained(e.tensor_tensor(f[1], fw[:, :, 1], bw[:, ::-1, 1], ALU.add))
            chained(e.tensor_tensor(f[1], f[1], av[:, :, 1], ALU.subtract))
            chained(e.tensor_tensor(f[2], f[0], f[0], ALU.mult))
            chained(e.tensor_tensor(f[3], f[1], f[1], ALU.mult))
            chained(e.tensor_tensor(f[2], f[2], f[3], ALU.add))
            chained(e.reciprocal(f[4], f[2]))
            chained(e.tensor_tensor(f[5], f[0], f[4], ALU.mult))
            chained(e.scalar_tensor_tensor(out=f[6], in0=f[1], scalar=-1.0, in1=f[4], op0=ALU.mult, op1=ALU.mult))
            chained(e.tensor_scalar(feat[:, 5:7, :], feat[:, 5:7, :], FEAT_MAX, -FEAT_MAX, ALU.min, ALU.max))
            chained(e.tensor_copy(fea[:, 0:2, :], feat[:, 5:7, :]))
            chained(e.tensor_tensor(fea[:, 3:5, :], feat[:, 5:7, :], fea[:, 0:2, :], ALU.subtract))
            chained(e.tensor_copy(fea[:, 6:8, :], fea[:, 0:2, :]))
            for j, one in ((2, 1.0), (5, 0.0), (8, 1.0)):
                e.memset(fea[:, j, :].bitcast(F32), one).then_inc(sem("feats"), 1)
            e.wait_ge(sem("sp_in"), 32)
            for n_, ins_ in enumerate((
                    lambda: e.tensor_tensor(spg[:, :], spw[:, :], bks[:, :], ALU.mult),
                    lambda: e.tensor_copy(sph[:, :], spg[:, :]),
                    lambda: e.tensor_tensor(spl[:, :], spg[:, :], sph[:, :], ALU.subtract),
                    lambda: e.tensor_scalar(spl[:, :], spl[:, :], cst[0:FR, C_LOW:C_LOW + 1], None, ALU.mult),
                    lambda: e.scalar_tensor_tensor(out=sps[:, :], in0=sph[:, :], scalar=cst[0:FR, C_LOW + 1:C_LOW + 2],
                                                   in1=spl[:, :], op0=ALU.mult, op1=ALU.add))):
                ins_().then_inc(sem("spg"), 1)
                e.wait_ge(sem("spg"), n_ + 1)
            e.wait_ge(sem("wabs"), 4)
            e.tensor_scalar(wqr[:, :, :, :], wqr[:, :, :, :], 0.0, 0.5, ALU.is_ge, ALU.subtract).then_inc(sem("signs0"), 1)
            e.tensor_scalar(wvr[:, :, :], wvr[:, :, :], 0.0, 0.5, ALU.is_ge, ALU.subtract).then_inc(sem("signs0"), 1)
            e.wait_ge(sem("signs0"), 2)
            e.wait_ge(sem("abs_sum"), 1)
            for c in range(2):
                two = lambda w: w[:, c, :, :].rearrange("p (b j) o -> p b (j o)", b=2)
                e.scalar_tensor_tensor(out=two(wqh), in0=ps[:, 0:2, 0:G * P], scalar=0.0, in1=two(wqr),
                                       op0=ALU.is_gt, op1=ALU.mult).then_inc(sem("signs"), 1)
                e.scalar_tensor_tensor(out=wvh[:, c, :], in0=ps[:, 2, 0:D], scalar=0.0, in1=wvr[:, c, :],
                                       op0=ALU.is_gt, op1=ALU.mult).then_inc(sem("signs"), 1)
            e.tensor_scalar(wprb[:, :, :], wraw[:, :, :], 0.0, 0.5, ALU.is_ge, ALU.subtract).then_inc(sem("signs"), 1)
            e.tensor_scalar(psc[:, :], ps[0:T, 3, 0:D], 4.0 / D, None, ALU.mult).then_inc(sem("psc"), 1)
            e.wait_ge(sem("h_in1"), 16)
            for j in range(S // 2):
                hj = H[:, 2 * j * D:2 * (j + 1) * D]
                e.wait_ge(sem("sp_mm"), j + 1)
                e.tensor_tensor(hj, hj, ps[0:T, 4 + j % 4, 0:2 * D], ALU.add).then_inc(sem("sp_add"), 1)
            e.wait_ge(sem("sp_add"), S // 2)
            e.wait_ge(sem("psc"), 1)
            e.wait_ge(sem("vb_set"), UA)

        KB = 2 * S

        def route_vector(e, L):
            seq = [0]

            def chained(ins_):
                seq[0] += 1
                ins_.then_inc(sem(f"r_dve{L}"), 1)
                e.wait_ge(sem(f"r_dve{L}"), seq[0])

            def bc(x, axis, shape):
                return x.unsqueeze(axis).broadcast_to(shape)

            TSE, TES = [T, S, E], [T, E, S]
            seen(e, "a_gc", L, S)
            lg = lgt[:, :].rearrange("t (s e) -> t s e", e=E + 1)
            keys = bc(cst[0:T, C_KEY:C_KEY + E], 1, TSE)
            if L == 0:
                chained(e.tensor_scalar(vcol[:, :], lg[:, :, E], V_MAX, -V_MAX, ALU.min, ALU.max))
            chained(e.tensor_copy(lg2[:, :, :], lg[:, :, 0:E]))
            for c in range(2):
                chained(e.tensor_reduce(top[c][:, :], lg2[:, :, :], AX.X, ALU.max))
                chained(e.tensor_tensor(key[:, :, :], lg2[:, :, :], bc(top[c][:, :], 2, TSE), ALU.is_equal))
                chained(e.tensor_tensor(key[:, :, :], key[:, :, :], keys, ALU.mult))
                chained(e.tensor_reduce(kmx[c][:, :], key[:, :, :], AX.X, ALU.max))
                chained(e.tensor_tensor(sel[c][:, :, :], keys, bc(kmx[c][:, :], 2, TSE), ALU.is_equal))
                if c == 0:
                    chained(e.scalar_tensor_tensor(out=lg2[:, :, :], in0=sel[0][:, :, :], scalar=-3e38,
                                                   in1=lg2[:, :, :], op0=ALU.mult, op1=ALU.add))
            chained(e.tensor_tensor(msk[:, :, :].rearrange("t e s -> t s e"), sel[0][:, :, :], sel[1][:, :, :], ALU.add))
            e.tensor_tensor(wts[:, 0, :], top[1][:, :], top[0][:, :], ALU.subtract).then_inc(sem("r_gap"), 1)
            seen(e, "r_cnt", L, 1)
            within = ps[0:T, 0, 0:E * S]
            total = ps[0:T, 1, 0:E * S]
            inc2 = incl[:, :, :].rearrange("t e s -> t (e s)")
            chained(e.tensor_tensor_scan(inc2, cst[0:T, C_RST:C_RST + E * S], total, 0.0, ALU.mult, ALU.add))
            chained(e.tensor_tensor(ceil[:, :, :], bc(incl[:, :, S - 1], 2, [T, E, NCEIL]),
                                    bc(cst[0:T, C_CEIL:C_CEIL + NCEIL], 1, [T, E, NCEIL]), ALU.is_gt))
            chained(e.tensor_reduce(cnt[:, 0, :], ceil[:, :, :], AX.X, ALU.add))
            chained(e.tensor_tensor_scan(cnt[:, 1, :], cst[0:T, C_ONE:C_ONE + E], cnt[:, 0, :], 0.0, ALU.mult, ALU.add))
            chained(e.tensor_tensor(cnt[:, 2, :], cnt[:, 1, :], cnt[:, 0, :], ALU.subtract))
            chained(e.tensor_scalar(cnt[:, 3, :], cnt[:, 2, :], float(P), None, ALU.mult))
            pos2 = pos[:, :, :].rearrange("t e s -> t (e s)")
            chained(e.tensor_tensor(pos2, inc2, total, ALU.subtract))
            chained(e.tensor_tensor(pos2, pos2, within, ALU.add))
            chained(e.tensor_tensor(pos[:, :, :], pos[:, :, :], bc(cnt[:, 3, :], 2, TES), ALU.add))
            for c in range(2):
                chained(e.tensor_tensor(key[:, :, :], sel[c][:, :, :], pos[:, :, :].rearrange("t e s -> t s e"), ALU.mult))
                chained(e.tensor_reduce(slot[:, c, :], key[:, :, :], AX.X, ALU.add))
            chained(e.tensor_copy(sli[:, 0, :], slot[:, :, :].rearrange("t c s -> t (c s)")))
            chained(e.tensor_scalar(sli[:, 1, :], sli[:, 0, :], 7, None, ALU.logical_shift_right))
            chained(e.tensor_scalar(sli[:, 2, :], sli[:, 0, :], P - 1, None, ALU.bitwise_and))
            chained(e.tensor_copy(hilo[:, :, :], sli[:, 1:3, :]))
            chained(e.tensor_tensor(et[:, :, :], bc(cst[0:1, C_IOT:C_IOT + TILES], 2, [1, TILES, E]),
                                    bc(cnt[0:1, 1, :], 1, [1, TILES, E]), ALU.is_ge))
            chained(e.tensor_reduce(etf[:, :], et[:, :, :], AX.X, ALU.add))
            chained(e.tensor_scalar(eti[:, :], etf[:, :], float(E - 1), None, ALU.min))
            for c in range(KB // CK):
                p = c % 2
                ksl = slice(c * CK, (c + 1) * CK)
                if c >= 2:
                    seen(e, "r_oh", L, c - 1)
                e.tensor_tensor(ohl[p][:, :, :], bc(cst[0:T, C_IOTA:C_IOTA + P], 1, [T, CK, P]),
                                bc(hilo[:, 1, ksl], 2, [T, CK, P]), ALU.is_equal).then_inc(sem("r_l"), 1)
                if c >= 2:
                    seen(e, "r_i", L, c - 1)
                e.tensor_tensor(ohh[p][:, :, :], bc(cst[0:T, C_IOT:C_IOT + TILES], 1, [T, CK, TILES]),
                                bc(hilo[:, 0, ksl], 2, [T, CK, TILES]), ALU.is_equal).then_inc(sem("r_h"), 1)
                seen(e, "r_h", L, 2 * c + 1)
                e.tensor_scalar(oht[p][:, :, 0, :], ohh[p][:, :, :], cst[0:T, C_P1:C_P1 + 1], None,
                                ALU.mult).then_inc(sem("r_h"), 1)
            seen(e, "r_oh", L, KB // CK)
            chained(e.tensor_copy(tks[:, :, :], ps[:, 5, 0:2 * TILES].rearrange("p (a j) -> p a j", a=2)))
            chained(e.tensor_scalar(used[:, :], tks[:, 0, :], 1.0, None, ALU.min))
            chained(e.scalar_tensor_tensor(out=tid[:, :], in0=tks[:, 1, :], scalar=float(T), in1=tks[:, 0, :],
                                           op0=ALU.mult, op1=ALU.add))
            chained(e.tensor_tensor(gidx[:, :], tid[:, :], used[:, :], ALU.subtract))
            chained(e.tensor_scalar(used[:, :], used[:, :], -UNUSED - 1.0, float(UNUSED), ALU.mult, ALU.add))
            chained(e.tensor_tensor(sidx[:, :], tid[:, :], used[:, :], ALU.add))
            return seq[0]

        def route_tensor(e, L):
            e.wait_ge(sem("masks"), 2)
            seen(e, "r_gap", L, 1)
            m = msk[:, :, :].rearrange("t e s -> t (e s)")
            e.matmul(ps[0:T, 0, 0:E * S], tri_bf[0:T, 0:T], m, start=True, stop=True)
            e.matmul(ps[0:T, 1, 0:E * S], ones_bf[0:T, 0:T], m, start=True, stop=True).then_inc(sem("r_cnt"), 1)
            if L == 0:
                e.matmul(ps[0:S, 6, 0:T], vcol[:, :], eye[0:T, 0:T], start=True, stop=True)
                e.matmul(ps[S:2 * S, 6, 0:T], vcol[:, :], cst[0:T, C_REV:C_REV + T], start=True,
                         stop=True).then_inc(sem("vrow"), 1)
            for c in range(KB // CK):
                seen(e, "r_l", L, c + 1)
                seen(e, "r_h", L, 2 * c + 2)
                seen(e, "r_i", L, c + 1)
                for q in range(CK):
                    j = c * CK + q
                    mm = e.matmul(ps[:, 5, 0:2 * TILES], ohl[c % 2][:, q, :],
                                  oht[c % 2][:, q, :, :].rearrange("t a j -> t (a j)"),
                                  start=(j == 0), stop=(j == KB - 1))
                mm.then_inc(sem("r_oh"), 1)

        def choice_scalar(e, L):
            seen(e, "r_gap", L, 1)
            e.activation(wts[:, 1, :], wts[:, 0, :], ACT.Exp).then_inc(sem("r_exp"), 1)

        def image_scalar(e, L):
            for c in range(KB // CK):
                seen(e, "r_h", L, 2 * c + 1)
                if c >= 2:
                    seen(e, "r_oh", L, c - 1)
                for q in range(CK):
                    img = e.mul(oht[c % 2][:, q, 1, :], ohh[c % 2][:, q, :], float((c * CK + q) % S))
                img.then_inc(sem("r_i"), 1)

        def route_pool(e, L):
            seen(e, "r_exp", L, 1)
            seq = [0]

            def chained(ins_):
                seq[0] += 1
                ins_.then_inc(sem("r_cw"), 1)
                seen(e, "r_cw", L, seq[0])
            at_e = lambda w: w.unsqueeze(2).broadcast_to([T, S, E])
            one = cst[0:T, C_ONE:C_ONE + S]
            chained(e.tensor_tensor(wts[:, 2, :], wts[:, 1, :], one, ALU.add))
            chained(e.tensor_tensor(wts[:, 2, :], wts[:, 2, :], wts[:, 2, :], ALU.mult))
            chained(e.tensor_tensor(wts[:, 2, :], wts[:, 2, :], cst[0:T, C_NHALF:C_NHALF + S], ALU.pow))
            chained(e.tensor_tensor(wts[:, 3, :], wts[:, 1, :], wts[:, 2, :], ALU.mult))
            chained(e.tensor_tensor(comb[:, :, :], sel[0][:, :, :], at_e(wts[:, 2, :]), ALU.mult))
            chained(e.tensor_tensor(cmb2[:, :, :], sel[1][:, :, :], at_e(wts[:, 3, :]), ALU.mult))
            chained(e.tensor_tensor(comb[:, :, :], comb[:, :, :], cmb2[:, :, :], ALU.add))

        def route_sync(e, L):
            for p in range(UA):
                seen(e, f"st_x{p}", L, 16 * (S // UA))
            seen(e, "r_cw", L, 7)
            load(e, rows_d[L].rearrange("(s t) c -> t s c", t=T)[:, :, D + 1:D + 1 + E], comb[:, :, :], f"comb{L}")

        EXP = dict(first=-2, last=TILES - 1, whole=(4, TILES - 1 - 4), U=UM)

        def exp_pool(e, L):
            e.wait_ge(sem(f"comb{L}"), 16)
            for p in range(UA):
                seen(e, f"st_h{p}", L, 16 * (S // UA))
            e.wait_ge(sem(f"r_dve{L}"), ROUTE_ALL[L])
            bound = e.to_reg(N - 1)


            def copy_index(cur_, table, count, i):
                e.tensor_copy(cur_[i.par][:, :], at(table, i, 1)).then_inc(sem(count), 1)

            def gather(i):
                e.indirect_dma_start(out=xg[i.par][:, :], out_offset=None, in_=rows_d[L],
                                     in_offset=bass.IndirectOffsetOnAxis(ap=gcur[i.par][:, :], axis=0),
                                     bounds_check=bound, oob_is_err=False).then_inc(sem(f"m_g{i.par}"), 16)

            for c in range(UM):
                copy_index(gcur, gidx, "m_gi", Idx(0, c, UM))
            copy_index(scur, sidx, "m_si", Idx(0, 0, UM))
            for c in range(UM):
                seen(e, "m_gi", L, c + 1)
                gather(Idx(0, c, UM))
            seen(e, "m_g0", L, 16)
            copy_index(gcur, gidx, "m_gi", Idx(0, UM, UM))

            def step(k):
                seen(e, "m_yw", L, k.val + 1)
                i = k + UM
                if i.live(TILES):
                    seen(e, "m_gi", L, i.val + 1)
                    seen(e, "m_xT", L, k.val + 1)
                    if (i + 1).live(TILES):
                        seen(e, f"m_g{(k + 1).par}", L, 16 * ((k + 1).turn + 1))
                        copy_index(gcur, gidx, "m_gi", i + 1)
                    gather(i)
                i = k
                seen(e, "m_si", L, i.val + 1)
                if not i.first(1):
                    seen(e, "m_sc", L, 16 * i.val)
                if (k + 1).live(TILES):
                    copy_index(scur, sidx, "m_si", k + 1)
                e.indirect_dma_start(out=acc_d[L], out_offset=bass.IndirectOffsetOnAxis(ap=scur[i.par][:, :], axis=0),
                                     in_=yw[i.par][:, :], in_offset=None, bounds_check=bound, oob_is_err=False,
                                     compute_op=ALU.add).then_inc(sem("m_sc"), 16)
            steps(e, step, first=0, last=TILES - 1, whole=(4, TILES - 1 - 5), U=UM)
            seen(e, "m_sc", L, 16 * TILES)

        def expert_of(e, i):
            return e.value_load(eti[0:1, bass.ds(i.val, 1)], min_val=0, max_val=E - 1)

        def exp_tensor(e, L):
            e.wait_ge(sem(f"r_dve{L}"), ROUTE_ALL[L])
            e.wait_ge(sem(f"we_in{L}"), 48)
            e.wait_ge(sem("w1_lo"), E * (L + 1))
            w1l = w1[:, :, :].bitcast(F32R)
            known = {}

            def step(k):
                if k.live(TILES):
                    at_k = (id(k.m), k.c)
                    ex_dn = known.pop(at_k) if at_k in known else expert_of(e, k)
                if (k + 1).live(TILES):
                    ex_up = known[(id(k.m), k.c + 1)] = expert_of(e, k + 1)
                i = k
                if i.live(TILES):
                    seen(e, "m_act", L, 2 * i.val + 2)
                    for c in range(FC):
                        mm = e.transpose(ps[:, 2 + c // 3, (c % 3) * P:(c % 3 + 1) * P], hact[:, c * P:(c + 1) * P], eye)
                    mm.then_inc(sem("m_hT"), 1)
                i = k + 2
                if i.live(TILES):
                    seen(e, f"m_g{i.par}", L, 16 * (i.turn + 1))
                    if not i.first(1):
                        seen(e, "m_xl", L, i.val)
                    e.transpose(ps[0:HD, 5, 0:P], xg[i.par][:, 0:HD], eye)
                    e.transpose(ps[0:HD + 1, 5, P:2 * P], xg[i.par][:, HD:D + 1], eye).then_inc(sem("m_xT"), 1)
                i = k + 1
                if i.live(TILES):
                    seen(e, "m_xl", L, i.val + 1)
                    for b in range(2):
                        n_ = 0
                        for x_, w_ in ((xgTh, w1h), (xgTl, w1h), (xgTh, w1l)):
                            for c in range(2):
                                kk = HD + c
                                w = w_[0:kk, c, bass.ds(ex_up * F + b * (F // 2), F // 2)]
                                mm = e.matmul(ps[:, b, 0:F // 2], x_[i.par][0:kk, c, :], w, start=(n_ == 0), stop=(n_ == 5))
                                n_ += 1
                        mm.then_inc(sem("m_up"), 1)
                i = k
                if i.live(TILES):
                    seen(e, "m_hc", L, i.val + 1)
                    seen(e, "m_hd", L, i.val + 1)
                    if not i.first(1):
                        seen(e, "m_y", L, i.val)
                    w2f = w2[:, :, :].rearrange("p c d -> p (c d)")
                    for c in range(FC):
                        mm = e.matmul(ps[:, 4, 0:D], hTs[:, c, :], w2f[:, bass.ds(ex_dn * (FC * D) + c * D, D)],
                                      start=(c == 0), stop=(c == FC - 1))
                    mm.then_inc(sem("m_dn"), 1)
            steps(e, step, first=-2, last=TILES - 1, whole=(8, TILES - 1 - 2), U=2 * UM, B=UM)

        def split_scalar(e, L, experts):
            e.wait_ge(sem(f"we_in{L}"), 48)
            seen(e, "a_gc", L, S)
            for x in experts:
                e.copy(w1h[:, :, x * F:(x + 1) * F], w1[:, :, x * F:(x + 1) * F]).then_inc(sem("w1_hi"), 1)

        def split_pool(e, L, experts):
            for x in experts:
                e.wait_ge(sem("w1_hi"), E * L + x + 1)
                w = w1[:, :, x * F:(x + 1) * F]
                e.tensor_tensor(w.bitcast(F32R), w, w1h[:, :, x * F:(x + 1) * F], ALU.subtract).then_inc(sem("w1_lo"), 1)

        def exp_scalar(e, L):
            func = ACT.Gelu_apprx_tanh if L == 0 else ACT.Relu

            def step(k):
                i = k
                if i.live(TILES):
                    seen(e, "m_hT", L, i.val + 1)
                    if not i.first(1):
                        seen(e, "m_dn", L, i.val)
                    e.copy(hTs[:, 0:3, :], ps[:, 2, 0:3 * P].rearrange("p (c t) -> p c t", c=3)).then_inc(sem("m_hc"), 1)
                i = k + 2
                if i.live(TILES):
                    seen(e, "m_xT", L, i.val + 1)
                    if not i.first(UM):
                        seen(e, "m_up", L, 2 * (i.val - 3))
                    src = ps[:, 5, 0:2 * P].rearrange("p (c t) -> p c t", c=2)
                    e.copy(xgTh[i.par][0:HD, 0, :], src[0:HD, 0, :]).then_inc(sem("m_xc"), 1)
                    e.copy(xgTh[i.par][:, 1, :], src[0:HD + 1, 1, :]).then_inc(sem("m_xc"), 1)
                i = k + 1
                if i.live(TILES):
                    for b in range(2):
                        seen(e, "m_up", L, 2 * i.val + b + 1)
                        if b == 0 and not i.first(1):
                            seen(e, "m_hT", L, i.val)
                        e.activation(hact[:, b * (F // 2):(b + 1) * (F // 2)], ps[:, b, 0:F // 2], func
                                     ).then_inc(sem("m_act"), 1)
            steps(e, step, **EXP)

        def exp_vector(e, L):
            if L == 0:
                e.wait_ge(sem("vrow"), 1)
                a3 = avec[:, :].rearrange("s (t c) -> s t c", c=2)
                e.memset(a3[:, :, 1], -1.0).then_inc(sem("chain"), 1)
                e.scalar_tensor_tensor(out=a3[:, :, 0], in0=ps[0:2 * S, 6, 0:T], scalar=-2.0,
                                       in1=cst[0:2 * S, C_ALT:C_ALT + T], op0=ALU.add, op1=ALU.mult
                                       ).then_inc(sem("chain"), 1)
                e.wait_ge(sem("chain"), 2)
                e.tensor_copy(cur[0][:, :], avec[:, 0:2]).then_inc(sem("chain"), 1)
                e.tensor_copy(xy[:, 0:2], avec[:, 0:2]).then_inc(sem("chain0"), 1)
            e.wait_ge(sem(f"we_in{L}"), 48)

            def chain(k, u):
                t = 2 * k.val + u + 1
                done = 4 * (2 * k.val + u) + 3
                a, b = cur[u], cur[1 - u]
                e.wait_ge(sem("chain"), done)
                e.tensor_tensor_reduce(sqj[:, :], a[:, :], a[:, :], 1.0, 0.0, ALU.mult, ALU.add,
                                       nrm[:, 0:1]).then_inc(sem("chain"), 1)
                e.wait_ge(sem("chain"), done + 1)
                e.reciprocal(nrm[:, 1:2], nrm[:, 0:1]).then_inc(sem("chain"), 1)
                e.wait_ge(sem("chain"), done + 2)
                e.scalar_tensor_tensor(out=b[:, :], in0=a[:, :], scalar=nrm[:, 1:2], in1=avec[:, bass.ds(2 * t, 2)],
                                       op0=ALU.mult, op1=ALU.add).then_inc(sem("chain"), 1)
                e.wait_ge(sem("chain"), done + 3)
                e.tensor_copy(xy[:, bass.ds(2 * t, 2)], b[:, :]).then_inc(sem("chain"), 1)

            def low(i):
                if i.live(TILES):
                    seen(e, "m_xc", L, 2 * i.val + 2)
                    src = ps[:, 5, 0:2 * P].rearrange("p (c t) -> p c t", c=2)
                    e.tensor_tensor(xgTl[i.par][0:HD, 0, :], src[0:HD, 0, :], xgTh[i.par][0:HD, 0, :], ALU.subtract)
                    e.tensor_tensor(xgTl[i.par][:, 1, :], src[0:HD + 1, 1, :], xgTh[i.par][:, 1, :],
                                    ALU.subtract).then_inc(sem("m_xl"), 1)
            low(Idx(0, 0, UM))
            low(Idx(0, 1, UM))

            def step(k, with_chain):
                low(k + 2)
                i = k
                seen(e, "m_hT", L, i.val + 1)
                if not i.first(1):
                    seen(e, "m_dn", L, i.val)
                e.tensor_copy(hTs[:, 3:, :], ps[:, 3, 0:3 * P].rearrange("p (c t) -> p c t", c=3)).then_inc(sem("m_hd"), 1)
                if with_chain:
                    chain(k, 0)
                    chain(k, 1)
                ex = expert_of(e, i)
                seen(e, "m_dn", L, i.val + 1)
                e.tensor_tensor(yb[:, :], ps[:, 4, 0:D], b2[:, bass.ds(ex * D, D)], ALU.add).then_inc(sem("m_y"), 1)
                seen(e, "m_y", L, i.val + 1)
                if not i.first(UM):
                    seen(e, "m_sc", L, 16 * (i.val - 3))
                e.tensor_scalar(yw[i.par][:, :], yb[:, :], xg[i.par][:, bass.ds(ex + (D + 1), 1)], None,
                                ALU.mult).then_inc(sem("m_yw"), 1)
            if L == 0:
                assert CHAIN_TILES % UM == 0 and CHAIN_PER_TILE * CHAIN_TILES == T - 1
                steps(e, lambda k: step(k, True), first=0, last=CHAIN_TILES - 1, whole=(UM, CHAIN_TILES - 1), U=UM)
                for k in range(CHAIN_TILES, TILES):
                    step(Idx(0, k, UM), False)
            else:
                steps(e, lambda k: step(k, False), first=0, last=TILES - 1, whole=(4, TILES - 1 - 4), U=UM)

        ROUTE_ALL = {}

        @block.vector
        def _(e):
            tok_vector(e)
            for L in range(2):
                att_vector(e, L)
                ROUTE_ALL[L] = route_vector(e, L)
                exp_vector(e, L)

        @block.scalar
        def _(e):
            tok_scalar(e)
            for L in range(2):
                att_scalar(e, L)
                split_scalar(e, L, range(0, E // 2))
                choice_scalar(e, L)
                split_scalar(e, L, range(E // 2, E))
                image_scalar(e, L)
                exp_scalar(e, L)

        @block.tensor
        def _(e):
            tok_tensor(e)
            for L in range(2):
                att_tensor(e, L)
                route_tensor(e, L)
                exp_tensor(e, L)

        @block.gpsimd
        def _(e):
            tok_pool(e)
            for L in range(2):
                att_pool(e, L)
                split_pool(e, L, range(0, 3))
                route_pool(e, L)
                split_pool(e, L, range(3, E))
                exp_pool(e, L)

        @block.sync
        def _(e):
            tok_sync(e)
            for L in range(2):
                att_sync(e, L)
                route_sync(e, L)


def _constants():
    import numpy as np
    c = np.zeros((P, C_END), np.float32)
    p = np.arange(P)
    c[:, C_EYE:C_EYE + P] = np.eye(P)
    c[:, C_TRI:C_TRI + P] = p[:, None] < p[None, :]
    c[:, C_ONE:C_ONE + P] = 1
    c[:, C_IOTA:C_IOTA + P] = p
    c[:T, C_REV:C_REV + T] = np.eye(T)[::-1]
    c[:, C_P1] = p + 1
    c[:, C_IOT:C_IOT + TILES] = np.arange(TILES)
    c[:, C_KEY:C_KEY + E] = E - np.arange(E)
    c[:, C_CEIL:C_CEIL + NCEIL] = P * np.arange(NCEIL)
    c[:, C_RST:C_RST + E * S] = np.tile(np.arange(S) > 0, E)
    c[:, C_ALT:C_ALT + T] = 1 - 2 * (np.arange(T) % 2)
    c[:, C_NHALF:C_NHALF + S] = -0.5
    c[S:2 * S, C_SEL:C_SEL + S] = np.eye(S)
    c[FR - 3:FR, C_LOW] = 1
    c[:, C_HALF] = np.where(p % 32 < DH, 0.5, 1)
    c[0:FR - 3, C_LOW + 1] = 1
    return c


def _rim(a, fill=0):
    import numpy as np
    q = PATCH
    lead = a.shape[:-3]
    parts = (a[..., 1:q + 1, 1:q + 1, :], a[..., 0, 1:q + 1, :], a[..., q + 1, 1:q + 1, :],
             a[..., 1:q + 1, 0, :], a[..., 1:q + 1, q + 1, :])
    return np.concatenate([x.reshape(*lead, -1) for x in parts], axis=-1)


def _layout(a):
    import numpy as np
    q = PATCH
    z = lambda *s: np.zeros(s, np.float32)
    out = {"consts": _constants()}
    x = z(S, 98, 98, CH)
    x[:, 1:-1, 1:-1] = a["x"]
    win = np.stack([np.stack([x[:, h * q:h * q + q + 2, w * q:w * q + q + 2] for w in range(6)], 1)
                    for h in range(6)], 1)
    out["pixels"] = _rim(win).reshape(S * NPATCH, NPIX)
    off = [(0, 0), (0, -1), (0, 1), (-1, 0), (1, 0)]

    def spread(v):
        v = v.reshape(q, q, SHIFTS, CH, -1)
        r = np.zeros((SHIFTS, v.shape[-1], q + 2, q + 2, CH), v.dtype)
        for s, (di, dj) in enumerate(off):
            r[s, :, 1 + di:1 + di + q, 1 + dj:1 + dj + q] = v[:, :, s].transpose(3, 0, 1, 2)
        return _rim(r).transpose(0, 2, 1)

    cols = lambda v: np.ascontiguousarray(v.reshape(SHIFTS, NK, KP, -1).transpose(0, 2, 1, 3))
    out["tok_w"] = cols(spread(a["L0_tok_W"]))
    gb = [cols(spread(a[k][:, None]))[..., 0].transpose(1, 0, 2) for k in ("L0_tok_gamma", "L0_tok_beta")]
    out["tok_gb"] = np.ascontiguousarray(np.stack(gb, 1))
    one = np.ones((q * q * SHIFTS * CH, 1), np.int64)
    m = spread(one)[..., 0]
    out["mult"] = np.tile((m > 0).sum(0).astype(np.float32)[None], (P, 1))
    out["L0_tok_b"] = a["L0_tok_b"]
    out["txt"] = a["txt"]
    halves = lambda w: np.ascontiguousarray(w.reshape(2, HD, -1).transpose(1, 0, 2))
    for L in range(2):
        w = a[f"L{L}_attn_w_qkv"].reshape(3, G, R, DH, D)
        pad = z(2, G, R, 32, D)
        pad[:, :, :, :DH] = w[:2]
        out[f"wqk{L}"] = halves(pad.reshape(2 * G * P, D).T).reshape(HD, 2, 2 * G, P)
        out[f"wv{L}"] = halves(w[2].reshape(D, D).T)
        for k in (f"wqk{L}", f"wv{L}"):
            out[k] = np.concatenate([out[k], z(P - HD, *out[k].shape[1:])])
        wp = a[f"L{L}_attn_w_proj"].T
        if L == 0:
            out["wpr0"] = halves(wp)
        else:
            pad = z(G, R, 32, D)
            pad[:, :, :DH] = wp.reshape(G, R, DH, D)
            out["wpr1"] = np.ascontiguousarray(pad.reshape(G, P, D).transpose(1, 0, 2))
        out[f"bpr{L}"] = np.tile(a[f"L{L}_attn_b_proj"][None], (T, 1))
        g = z(D + 2, E + 1)
        if L == 0:
            g[:D, :E] = a["L0_ffn_gate_w"]
            g[:D, E] = a["L0_ffn_v_w"]
            g[D, :E] = a["L0_ffn_gate_b"]
            g[D, E] = a["L0_ffn_v_b"]
        else:
            g[:D, :E] = a["L1_ffn_Wr"]
        wg = z(HD + 1, 2, E + 1)
        wg[:HD, 0], wg[:, 1] = g[:HD], g[HD:D + 1]
        out[f"wg{L}"] = wg
        u1, c1, u2, c2 = [a[f"L0_ffn_{k}" if L == 0 else f"L1_ffn_{k}"] for k in
                          (("w1", "b1", "w2", "b2") if L == 0 else ("W1", "b1", "W2", "b2"))]
        wu = z(HD + 1, 2, E, F)
        wu[:HD] = u1.reshape(E, 2, HD, F).transpose(2, 1, 0, 3)
        wu[HD, 1] = c1
        out[f"w1_{L}"] = wu.reshape(HD + 1, 2, E * F)
        out[f"w2_{L}"] = np.ascontiguousarray(u2.reshape(E * FC, P, D).transpose(1, 0, 2))
        out[f"b2_{L}"] = np.tile(c2.reshape(1, E * D), (P, 1))
    out["spec_w"] = np.tile(np.concatenate([a["L0_ffn_out_w"], a["L0_ffn_out_b"][None]], 0), (FR // 3, 1))
    out["spec_s"] = np.tile(a["L0_ffn_bk_scale"][None], (FR, 1))
    return {k: np.ascontiguousarray(v) for k, v in out.items()}


def kernel(**inputs):
    import numpy as np
    import concourse.bacc as bacc
    from concourse.bass_utils import run_bass_kernel_spmd

    laid = _layout({k: np.asarray(v) for k, v in inputs.items()})
    nc = bacc.Bacc("TRN2", target_bir_lowering=False, num_devices=1)
    arrays, aps = {}, {}
    for name, v in laid.items():
        arrays[f"in_{name}"] = v
        aps[name] = nc.dram_tensor(f"in_{name}", v.shape, mybir.dt.from_np(v.dtype), kind="ExternalInput").ap()
    out = nc.dram_tensor("out", (S, T, D), F32, kind="ExternalOutput").ap()
    fusion_kernel(nc, aps, out)
    r = run_bass_kernel_spmd(nc, [arrays], core_ids=[0])
    return r.results[0]["out"]
```
